# Optimizing a Trainium2 kernel written in Bass

```python
import numpy as np
import jax
import jax.numpy as jnp

def _softmax(x, axis=-1):
    return jax.nn.softmax(x, axis=axis)

def _gelu(x):
    return jax.nn.gelu(x, approximate=True)

def _silu(x):
    return jax.nn.silu(x)

def _sigmoid(x):
    return jax.nn.sigmoid(x)

def _layernorm(x, axis=-1, eps=1e-05):
    m = jnp.mean(x, axis=axis, keepdims=True)
    v = jnp.var(x, axis=axis, keepdims=True)
    return (x - m) / jnp.sqrt(v + eps)

def _scatter_add(tgt, idx, src, axis=0):
    return tgt.at[idx].add(src)

def _segment_sum(src, seg, n):
    return jax.ops.segment_sum(src, seg, n)
kernel_name = 'mk_seq_preln_d1_jaxref_r8_412ad1'

def setup_inputs(seed: int=0):
    np.random.seed(seed)
    _w = jnp.asarray

    def _L0_attn_setup():
        import jax, jax.numpy as jnp
        import numpy as np
        HIDDEN = 256
        N_HEADS = 16
        HEAD_DIM = HIDDEN // N_HEADS

        def rotate_half(x):
            x1, x2 = jnp.split(x, 2, axis=-1)
            return jnp.concatenate([-x2, x1], axis=-1)
        key = jax.random.key(seed)
        k0, k1, k2, k3, k4 = jax.random.split(key, 5)
        B, S = (1, 256)
        scale = 1.0 / np.sqrt(HIDDEN)
        return {'hidden_states': jax.random.normal(k0, (B, S, HIDDEN), dtype=jnp.float32), 'Wq': jax.random.normal(k1, (HIDDEN, HIDDEN), dtype=jnp.float32) * scale, 'Wk': jax.random.normal(k2, (HIDDEN, HIDDEN), dtype=jnp.float32) * scale, 'Wv': jax.random.normal(k3, (HIDDEN, HIDDEN), dtype=jnp.float32) * scale, 'Wo': jax.random.normal(k4, (HIDDEN, HIDDEN), dtype=jnp.float32) * scale, 'gate': jnp.zeros((1, N_HEADS, 1, 1), dtype=jnp.float32)}
    _L0_attn_in = _L0_attn_setup()

    def _L0_ffn_setup():
        import jax, jax.numpy as jnp
        import numpy as np
        B, S, H, F, E, K = (2, 128, 256, 688, 8, 2)
        key = jax.random.key(seed)
        k0, k1, k2, k3, k4 = jax.random.split(key, 5)
        x = jax.random.normal(k0, (B, S, H), dtype=jnp.float32)
        router_w = jax.random.normal(k1, (E, H), dtype=jnp.float32) * 0.02
        gate_w = jax.random.normal(k2, (E, F, H), dtype=jnp.float32) * 0.02
        up_w = jax.random.normal(k3, (E, F, H), dtype=jnp.float32) * 0.02
        down_w = jax.random.normal(k4, (E, H, F), dtype=jnp.float32) * 0.02
        return {'x': x, 'router_w': router_w, 'gate_w': gate_w, 'up_w': up_w, 'down_w': down_w}
    _L0_ffn_in = _L0_ffn_setup()
    _d = {'L0_attn_hidden_states': _L0_attn_in['hidden_states'], 'L0_attn_Wq': _L0_attn_in['Wq'], 'L0_attn_Wk': _L0_attn_in['Wk'], 'L0_attn_Wv': _L0_attn_in['Wv'], 'L0_attn_Wo': _L0_attn_in['Wo'], 'L0_attn_gate': _L0_attn_in['gate'], 'L0_ffn_router_w': _L0_ffn_in['router_w'], 'L0_ffn_gate_w': _L0_ffn_in['gate_w'], 'L0_ffn_up_w': _L0_ffn_in['up_w'], 'L0_ffn_down_w': _L0_ffn_in['down_w']}
    _x0 = _d['L0_attn_hidden_states']
    _d['L0_attn_hidden_states'] = jax.random.normal(jax.random.fold_in(jax.random.key(seed), 1), (1, 1024, 256), dtype=_x0.dtype)
    del _x0
    return _d

def reference(L0_attn_hidden_states, L0_attn_Wq, L0_attn_Wk, L0_attn_Wv, L0_attn_Wo, L0_attn_gate, L0_ffn_router_w, L0_ffn_gate_w, L0_ffn_up_w, L0_ffn_down_w):

    def _L0_attn_ref(hidden_states, Wq, Wk, Wv, Wo, gate):
        import jax, jax.numpy as jnp
        import numpy as np
        HIDDEN = 256
        N_HEADS = 16
        HEAD_DIM = HIDDEN // N_HEADS

        def rotate_half(x):
            x1, x2 = jnp.split(x, 2, axis=-1)
            return jnp.concatenate([-x2, x1], axis=-1)
        B, S, H = hidden_states.shape
        q = hidden_states @ Wq.T
        k = hidden_states @ Wk.T
        v = hidden_states @ Wv.T
        inv_freq = 1.0 / 10000.0 ** (jnp.arange(0, H, 2, dtype=jnp.float32) / H)
        t = jnp.arange(S, dtype=jnp.float32)
        freqs = t[:, None] * inv_freq[None, :]
        emb = jnp.concatenate([freqs, freqs], axis=-1)[None]
        cos, sin = (jnp.cos(emb), jnp.sin(emb))
        q = q * cos + rotate_half(q) * sin
        k = k * cos + rotate_half(k) * sin

        def split_heads(x):
            return x.reshape(B, S, N_HEADS, HEAD_DIM).transpose(0, 2, 1, 3)
        q, k, v = (split_heads(q), split_heads(k), split_heads(v))
        k_feat = jax.nn.elu(k) + 1.0
        memory = jnp.einsum('bhsd,bhse->bhde', k_feat, v)
        norm_term = k_feat.sum(axis=2)
        q_feat = jax.nn.elu(q) + 1.0
        mem_out = jnp.einsum('bhsd,bhde->bhse', q_feat, memory)
        denom = jnp.einsum('bhsd,bhd->bhs', q_feat, norm_term)[..., None]
        mem_out = mem_out / denom
        scale = 1.0 / jnp.sqrt(jnp.float32(HEAD_DIM))
        scores = jnp.einsum('bhqd,bhkd->bhqk', q, k) * scale
        attn = jnp.einsum('bhqk,bhkd->bhqd', jax.nn.softmax(scores, axis=-1), v)
        g = jax.nn.sigmoid(gate)
        combined = g * mem_out + (1.0 - g) * attn
        combined = combined.transpose(0, 2, 1, 3).reshape(B, S, H)
        return combined @ Wo.T

    def _L0_ffn_ref(x, router_w, gate_w, up_w, down_w):
        import jax, jax.numpy as jnp
        import numpy as np
        B, S, H, F, E, K = (2, 128, 256, 688, 8, 2)
        b, s, h = x.shape
        xf = x.reshape(-1, h)
        logits = xf @ router_w.T
        top_v, top_i = jax.lax.top_k(logits, K)
        probs = jax.nn.softmax(top_v.astype(jnp.float32), axis=-1).astype(logits.dtype)
        combine = jnp.sum(jax.nn.one_hot(top_i, E, dtype=x.dtype) * probs[..., None], axis=1)
        g = jnp.einsum('th,efh->etf', xf, gate_w)
        u = jnp.einsum('th,efh->etf', xf, up_w)
        y = jnp.einsum('etf,ehf->eth', jax.nn.silu(g) * u, down_w)
        out = jnp.einsum('te,eth->th', combine, y)
        return out.reshape(b, s, h)
    x = L0_attn_hidden_states
    x = x + _L0_attn_ref(_layernorm(x, axis=-1), L0_attn_Wq, L0_attn_Wk, L0_attn_Wv, L0_attn_Wo, L0_attn_gate)
    x = x + _L0_ffn_ref(_layernorm(x, axis=-1), L0_ffn_router_w, L0_ffn_gate_w, L0_ffn_up_w, L0_ffn_down_w)
    return x

_drawn_inputs = setup_inputs


def setup_inputs(seed=0):
    import zlib

    import numpy as np

    out = dict(_drawn_inputs(seed))
    spreads = {'L0_attn_gate': (0.0, 0.8)}
    factors = {'L0_ffn_router_w': 3.276,
     'L0_ffn_gate_w': 2.879,
     'L0_ffn_up_w': 2.855,
     'L0_ffn_down_w': 2.86}
    for name, (base, spread) in spreads.items():
        noise = np.random.default_rng([zlib.crc32(name.encode()), seed]).standard_normal(out[name].shape)
        drawn = base * np.exp(spread * noise) if base else spread * noise
        out[name] = jnp.asarray(drawn.astype(out[name].dtype))
    for name, factor in factors.items():
        out[name] = (out[name] * factor).astype(out[name].dtype)
    return out
```

```python
from contextlib import ExitStack

import concourse.bass as bass
from concourse import mybir
from concourse.alu_op_type import AluOpType as ALU
import numpy as np

ACT = mybir.ActivationFunctionType
F32, BF16, U32, I32 = mybir.dt.float32, mybir.dt.bfloat16, mybir.dt.uint32, mybir.dt.int32
AX = mybir.AxisListType

P = 128
T, H, NH = 1024, 256, 16
HD = H // NH
TT, HB = T // P, H // P
HALF = T // 2
E, F, K = 8, 688, 2
FB = [P, P, P, P, 88, 88]
FO = [sum(FB[:i]) for i in range(len(FB))]
FN = F // 2
NTILE = (K * T + E * (P - 1)) // P
NSLOT = (NTILE + 1) * P
EPS = 1e-5
NQ = NH // 4
GROUPS = 6
QPART = [0, 0, 1, 1, 0, 2]
KPART = [0, 1, 0, 1, 2, 0]
SROWS = GROUPS * HD
QSTEP = 64
LEAD = 44

C_ID, C_MASK, C_TRI, C_LTI, C_J, C_IOTA, C_TAU = 0, 128, 256, 384, 448, 512, 520
NCONST = C_TAU + (NTILE + 1) * E


def constants():
    c = np.zeros((P, NCONST), np.float32)
    p = np.arange(P)
    c[:, C_ID:C_ID + P] = np.eye(P)
    c[:, C_MASK:C_MASK + P] = p[:, None] // HD == p[None] // HD
    c[:, C_TRI:C_TRI + P] = p[:, None] < p[None]
    e = np.arange(E)
    c[:, C_LTI:C_LTI + E * E] = (e[None] <= e[:, None]).reshape(-1)
    c[:, C_J:C_J + E * E] = np.tile(np.arange(T // P) * P, E)
    c[:, C_IOTA:C_IOTA + E] = e
    c[:, C_TAU:] = np.repeat(np.arange(NTILE + 1), E)
    inv_freq = np.float32(1) / np.float32(10000) ** (np.arange(0, H, 2, dtype=np.float32) / np.float32(H))
    angle = inv_freq[:, None] * np.arange(T, dtype=np.float32)[None]
    return c, np.stack([np.cos(angle), np.sin(angle)], 1).astype(np.float32)


def block_kernel(nc, x_d, w_d, rope_d, const_d, gate_d, router_d, gu_d, dn_d, out_d):
    ctx = ExitStack()
    with ctx:
        WORDS = 52000
        mem = ctx.enter_context(nc.sbuf_tensor("mem", [P, WORDS], F32))
        psum = ctx.enter_context(nc.psum_tensor("psum", [P, 8, 512], F32))

        def words(at, *shape, dt=F32, parts=P):
            n = int(np.prod(shape))
            v = mem[0:parts, at:at + (n if dt != BF16 else n // 2)]
            if dt != F32:
                v = v.bitcast(dt)
            names = "abcd"[:len(shape)]
            if len(shape) > 1:
                v = v.rearrange(f"p ({' '.join(names)}) -> p {' '.join(names)}",
                                **dict(zip(names, shape)))
            return v

        G = 0
        gu = words(G, HB, E, 2 * F)
        xn = words(G, TT, H)
        kfeat_tok = words(G, TT, H)
        xnT = words(G + 2048, HB, T)
        qfeat = words(G + 2048, HB, T)
        rope = words(G + 4096, 2, T)
        wqkv = words(G + 6144, 3, HB, H)
        kT = words(G + 7680, HB, T)
        qT = words(G + 9728, HB, T)
        parts = words(G + 11776, 2, 3, HB, T, dt=BF16)
        tmp = words(G + 17920, 4, HALF)
        kfeat = words(G + 19968, HB, T)
        A = HB * E * 2 * F
        dn = words(A, len(FB), E, H)
        qst = words(A, 2, 4, T, dt=BF16)
        kst = words(A + 4096, 2, 4, T, dt=BF16)
        prob = words(A + 8192, 8, HALF)
        resid = words(A + 8192, HB, 2, HALF)
        at = [A + len(FB) * E * H]

        def keep(*shape, dt=F32, parts=P):
            n = int(np.prod(shape))
            n = n if dt != BF16 else (n + 1) // 2
            v = words(at[0], *shape, dt=dt, parts=parts)
            at[0] += n
            return v

        x = keep(TT, H)
        b_v = at[0]
        v = keep(TT, H)
        vst = keep(TT, 4, 32)
        b_mem = at[0]
        memT = keep(HB, T)
        b_num = at[0]
        num = keep(HB, T)
        den = keep(HB, T)
        wo = keep(HB, H)
        const = keep(NCONST)
        ident_b = keep(P, dt=BF16)
        osb = keep(2, HALF)
        state = keep(HB, 2 * P)
        ones = keep(P)
        stat = keep(TT, 6)
        mv = keep(TT, 2)
        rstd = keep(TT)
        gate = keep(HB)
        gate_e = keep(HB)
        gate_1 = keep(HB)
        omg = keep(HB)
        half_c = keep(TT)
        mx = keep(2, 16)
        mhl = keep(2, 16, dt=BF16)
        mT = keep(P, dt=BF16, parts=32)
        router = keep(HB, E)
        lg = keep(TT, E)
        top = keep(TT, 8)
        topi = keep(TT, 8, dt=U32)
        topf = keep(TT, K)
        onehot = keep(K, TT, E)
        chosen = keep(TT, E, dt=BF16)
        tri_b = keep(P, dt=BF16)
        ones_b = keep(P, dt=BF16)
        pw = keep(K, TT)
        pw_d = keep(TT)
        pw_e = keep(TT)
        pw_s = keep(TT)
        cnt = keep(E)
        cmp = keep(E, E)
        tiles = keep(E)
        cum = keep(E)
        base = keep(E)
        base_t = keep(E)
        pos = keep(TT, E)
        sel = keep(K, TT, E)
        slot_f = keep(K, TT)
        slot = keep(K, TT, dt=U32)
        tau = keep(NTILE + 1, E)
        ex_f = keep(NTILE + 1)
        ex_i = keep(NTILE + 1, dt=I32)
        xg = keep(2, H)
        xgT = keep(2, HB, P)
        yt = keep(2, H)
        assert at[0] <= WORDS, at[0]
        xn2 = words(b_mem, TT, H)
        xn2T = words(b_v, HB, T)
        act_g = words(b_num, 2, F)
        hid = words(b_num + 2 * F, 2, F)
        hidT = words(b_v, 2, len(FB), P)
        gath = words(G, K, TT, H)
        ident = const[:, C_ID:C_ID + P]

        parts_d = nc.dram_tensor("parts_d", [2, 3, H, T], BF16).ap()
        max_d = nc.dram_tensor("max_d", [2 * NQ, 2, 4, HALF], BF16).ap()
        o_d = nc.dram_tensor("o_d", [2, NQ, P, HALF], F32).ap()
        xg_d = nc.dram_tensor("xg_d", [NSLOT, H], F32).ap()
        yg_d = nc.dram_tensor("yg_d", [NTILE * P, H], F32).ap()

        def sem(name):
            return ctx.enter_context(nc.semaphore(name))

        x_in = [sem(f"x_in{i}") for i in range(4)]
        w_in = [sem(f"w_in{i}") for i in range(3)]
        rope_in, const_in, gate_in, wo_in, router_in = (sem(n) for n in
            ("rope_in", "const_in", "gate_in", "wo_in", "router_in"))
        ones_set, vst_set, kst_set, zero_set = (sem(n) for n in ("ones_set", "vst_set", "kst_set", "zero_set"))
        xg_zero = sem("xg_zero")
        identb_ready = sem("identb_ready")
        dve_step = sem("dve_step")
        var_ready, rstd_ready, xn_ready, xnT_ps, xnT_ready = (sem(n) for n in
            ("var_ready", "rstd_ready", "xn_ready", "xnT_ps", "xnT_ready"))
        qk_ps, rope_mul, rope_ready = sem("qk_ps"), sem("rope_mul"), sem("rope_ready")
        hi_ready, res_ready, mid_ready, lo_ready = (sem(n) for n in ("hi_ready", "res_ready", "mid_ready", "lo_ready"))
        parts_out = sem("parts_out")
        v_ps, v_ready = sem("v_ps"), sem("v_ready")
        neg_ready, nexp_ready, feat_ready = sem("neg_ready"), sem("nexp_ready"), sem("feat_ready")
        kft_ps, kft_ready, st_ps, st_ready, lin_ps, lin_ready = (sem(n) for n in
            ("kft_ps", "kft_ready", "st_ps", "st_ready", "lin_ps", "lin_ready"))
        gexp_ready, gate_ready = sem("gexp_ready"), sem("gate_ready")
        stack_in = sem("stack_in")
        sc_ps, max_ready, mhl_ready, mT_ps, mT_ready = (sem(n) for n in
            ("sc_ps", "max_ready", "mhl_ready", "mT_ps", "mT_ready"))
        max_out, mrow_in = sem("max_out"), sem("mrow_in")
        sct_ps, exp_ready, av_ps, osb_ready = (sem(n) for n in ("sct_ps", "exp_ready", "av_ps", "osb_ready"))
        osb_out = [sem("osb_out0"), sem("osb_out1")]
        v_staged = sem("v_staged")
        num_in = [sem(f"num_in{i}") for i in range(4)]
        mix_ready = sem("mix_ready")
        wo_ps, x2_ready, xn2_ready, xn2T_ps, xn2T_ready = (sem(n) for n in
            ("wo_ps", "x2_ready", "xn2_ready", "xn2T_ps", "xn2T_ready"))
        lg_ps, top_ready, pexp_ready, chosen_ready, rank_ps, slot_ready, expert_ready = (sem(n) for n in
            ("lg_ps", "top_ready", "pexp_ready", "chosen_ready", "rank_ps", "slot_ready", "expert_ready"))
        scattered = sem("scattered")
        gu_in, dn_in = sem("gu_in"), sem("dn_in")
        xg_in = [sem("xg_in0"), sem("xg_in1")]
        xgT_ps, xgT_ready, gu_ps, silu_ready, hid_ready = (sem(n) for n in
            ("xgT_ps", "xgT_ready", "gu_ps", "silu_ready", "hid_ready"))
        hidT_ps, hidT_ready, y_ps, y_ready = (sem(n) for n in ("hidT_ps", "hidT_ready", "y_ps", "y_ready"))
        y_out = [sem("y_out0"), sem("y_out1")]
        gath_in = [sem(f"gath_in{i}") for i in range(TT)]
        out_ready, out_done = sem("out_ready"), sem("out_done")

        QK_IDX = [(w, hf) for hf in range(2) for w in range(2)]
        x_v = x_d.rearrange("o (n p) h -> p (o n) h", p=P)
        out_v = out_d.rearrange("o (n p) h -> p (o n) h", p=P)
        pv = parts_d.rearrange("w s (b p) t -> w s p b t", p=P)
        banks = lambda i, n: psum[:, i:i + n, :].rearrange("p b c -> p (b c)")

        def score_steps(more):
            out = []
            for t in range(QSTEP):
                s = t + LEAD
                nxt, s = s // QSTEP, s % QSTEP
                out.append((nxt, s) if not nxt or more else None)
            return out

        block = ctx.enter_context(nc.Block())

        @block.sync
        def _(sp):
            for i in range(4):
                sp.dma_start(x[:, 2 * i:2 * i + 2, :], x_v[:, 2 * i:2 * i + 2, :]).then_inc(x_in[i], 16)
                if i == 0:
                    sp.dma_start(const, const_d).then_inc(const_in, 16)
                    sp.dma_start(wqkv[:, 0], w_d[:, 0]).then_inc(w_in[0], 16)
            sp.dma_start(wo, w_d[:, 3]).then_inc(wo_in, 16)
            sp.dma_start(router, router_d).then_inc(router_in, 16)
            n = 0
            for i, (w, hf) in enumerate(QK_IDX):
                for s, ready in enumerate((hi_ready, mid_ready, lo_ready)):
                    sp.wait_ge(ready, i + 1)
                    sp.dma_start(pv[w, s][:, :, hf * HALF:(hf + 1) * HALF],
                                 parts[:, w, s, :, hf * HALF:(hf + 1) * HALF]).then_inc(parts_out, 16)
                    n += 16
            sp.wait_ge(parts_out, n)

            def stacks(qd, sl):
                for w, st, part in ((0, kst, KPART), (1, qst, QPART)):
                    for g in range(GROUPS):
                        src = parts_d[w, part[g]].rearrange("(q j r) t -> q r j t", j=4, r=HD)[qd]
                        sp.dma_start(st[g * HD:(g + 1) * HD, sl], src).then_inc(stack_in, 16)

            def max_rows(unit, sl, hf):
                sp.wait_ge(mT_ready, unit + 1)
                sp.dma_start(max_d[unit].rearrange("s j (b q) -> (s j b) q", b=4), mT).then_inc(max_out, 16)
                sp.wait_ge(max_out, 16 * (unit + 1))
                sp.dma_start(qst[SROWS:SROWS + 2, sl, :, hf * HALF:(hf + 1) * HALF],
                             max_d[unit]).then_inc(mrow_in, 16)

            def o_store(qd, hf):
                sp.wait_ge(osb_ready, 2 * qd + hf + 1)
                sp.dma_start(o_d[hf, qd], osb[:, hf]).then_inc(osb_out[hf], 16)

            stacks(0, 0)
            max_rows(0, 0, 0)

            def quad(qd, more):
                if more:
                    sp.wait_ge(exp_ready, QSTEP * qd)
                    sp.wait_ge(stack_in, 2 * GROUPS * 16 * (qd + 1))
                    stacks(qd + 1, (qd + 1) % 2)
                max_rows(2 * qd + 1, qd % 2, 1)
                o_store(qd, 0)
                if more:
                    max_rows(2 * qd + 2, (qd + 1) % 2, 0)
                o_store(qd, 1)

            with sp.Fori(0, NQ - 1) as qd:
                quad(qd, True)
            quad(NQ - 1, False)
            sp.wait_ge(xg_zero, 16)
            for hf in range(2):
                sp.wait_ge(osb_out[hf], 16 * NQ)
                for b in range(HB):
                    src = o_d[hf, 2 * b:2 * b + 2].rearrange("q (j r) t -> (q j) r t", r=32)
                    c = slice(hf * HALF, (hf + 1) * HALF)
                    sp.dma_start(num[:, b, c], src[:, 0:HD]).then_inc(num_in[2 * hf + b], 16)
                    sp.dma_start(den[:, b, c], src[:, HD:2 * HD]).then_inc(num_in[2 * hf + b], 16)
            sp.wait_ge(scattered, 16 * K * TT)

            def load_xg(t, par):
                sp.dma_start(xg[:, par], xg_d[bass.ts(t, P), :]).then_inc(xg_in[par], 16)

            def store_y(t, par):
                sp.wait_ge(y_ready, t + 1)
                sp.dma_start(yg_d[bass.ts(t, P), :], yt[:, par]).then_inc(y_out[par], 16)

            load_xg(0, 0)
            load_xg(1, 1)
            with sp.Fori(0, (NTILE - 1) // 2) as i:
                for r in (1, 2):
                    t = 2 * i + r
                    sp.wait_ge(xgT_ps, t)
                    load_xg(t + 1, (r + 1) % 2)
                    store_y(t - 1, (r + 1) % 2)
            store_y(NTILE - 1, (NTILE - 1) % 2)
            for n in range(TT):
                sp.wait_ge(out_ready, n + 1)
                sp.dma_start(out_v[:, n], x[:, n]).then_inc(out_done, 16)
            sp.wait_ge(out_done, 16 * TT)

        @block.gpsimd
        def _(pool):
            pool.memset(ones, 1.0).then_inc(ones_set, 1)
            pool.memset(half_c, -0.5).then_inc(ones_set, 1)
            pool.memset(vst[:, :, :, HD:], 1.0).then_inc(vst_set, 1)
            pool.memset(num[:, 0, 0:H], 0.0).then_inc(zero_set, 1)
            pool.wait_ge(ones_set, 2)
            pool.wait_ge(vst_set, 1)
            pool.wait_ge(zero_set, 1)
            pool.memset(kst[SROWS:SROWS + 2], -1.0).then_inc(kst_set, 1)
            pool.wait_ge(kst_set, 1)
            pool.dma_start(xg_d.rearrange("(n p) h -> p n h", p=P),
                           num[:, 0:1, 0:H].to_broadcast([P, NTILE + 1, H])).then_inc(xg_zero, 16)

            def reciprocal_root(g, n):
                pool.wait_ge(var_ready, g + 1)
                c = slice((g % n) * (TT // n), (g % n + 1) * (TT // n))
                nc.gpsimd.tensor_tensor(rstd[:, c], rstd[:, c], half_c[:, c], ALU.pow).then_inc(rstd_ready, 1)

            for g in range(4):
                reciprocal_root(g, 4)
            for i, (w, hf) in enumerate(QK_IDX):
                o, c = (kT, qT)[w], slice(hf * HALF, (hf + 1) * HALF)
                pool.wait_ge(rope_mul, i + 1)
                nc.gpsimd.tensor_tensor(o[:, 0, c], tmp[:, 0], tmp[:, 1], ALU.subtract)
                nc.gpsimd.tensor_tensor(o[:, 1, c], tmp[:, 2], tmp[:, 3], ALU.add).then_inc(rope_ready, 1)
            tv = tmp.rearrange("p (b h) c -> p b (h c)", b=HB)
            for i, src in enumerate((kT, qT)):
                if i == 0:
                    pool.wait_ge(rope_ready, 4)
                else:
                    pool.wait_ge(feat_ready, 1)
                nc.gpsimd.tensor_scalar(tv, src, 0.0, None, ALU.min).then_inc(neg_ready, 1)

            def stage_v(qd):
                pool.wait_ge(av_ps, 16 * qd)
                src = v.rearrange("p n (q c) -> p q n c", q=NQ)[:, qd].rearrange("p n (j c) -> p n j c", c=HD)
                nc.gpsimd.tensor_copy(vst[:, :, :, 0:HD], src).then_inc(v_staged, 1)

            pool.wait_ge(v_ready, 4)
            stage_v(0)
            pool.wait_ge(lin_ready, 4)
            pool.wait_ge(parts_out, 16 * 12)
            for e in range(E):
                pool.dma_start(gu[:, :, e, :], gu_d[:, :, e, :]).then_inc(gu_in, 16)
            with pool.Fori(1, NQ) as qd:
                stage_v(qd)
            reciprocal_root(4, 1)
            pool.wait_ge(av_ps, 16 * NQ)
            for c, (o, n) in enumerate(zip(FO, FB)):
                pool.dma_start(dn[0:n, c], dn_d[o:o + n]).then_inc(dn_in, 16)
            pool.wait_ge(xg_zero, 16)
            pool.wait_ge(slot_ready, 1)
            for k in range(K):
                for n in range(TT):
                    pool.indirect_dma_start(
                        out=xg_d, out_offset=bass.IndirectOffsetOnAxis(ap=slot[:, k, n:n + 1], axis=0),
                        in_=xn2[:, n], in_offset=None).then_inc(scattered, 16)
            for par in range(2):
                pool.wait_ge(y_out[par], 16 * ((NTILE + 1 - par) // 2))
            for n in range(TT):
                for k in range(K):
                    pool.indirect_dma_start(
                        out=gath[:, k, n], out_offset=None, in_=yg_d,
                        in_offset=bass.IndirectOffsetOnAxis(ap=slot[:, k, n:n + 1], axis=0)).then_inc(gath_in[n], 16)

        @block.scalar
        def _(act):
            act.dma_start(rope, rope_d).then_inc(rope_in, 16)
            act.dma_start(wqkv[:, 1], w_d[:, 1]).then_inc(w_in[1], 16)
            act.dma_start(wqkv[:, 2], w_d[:, 2]).then_inc(w_in[2], 16)
            act.dma_start(gate, gate_d).then_inc(gate_in, 16)
            act.wait_ge(gate_in, 16)
            nc.scalar.activation(gate_e, gate, ACT.Exp, scale=-1.0).then_inc(gexp_ready, 1)
            for hf in range(2):
                for b in range(HB):
                    act.wait_ge(xnT_ps, 2 * hf + b + 1)
                    nc.scalar.copy(xnT[:, b, hf * HALF:(hf + 1) * HALF], psum[:, 2 * hf + b]).then_inc(xnT_ready, 1)
            for i, (w, hf) in enumerate(QK_IDX):
                src, c = (kT, qT)[w][:, :, hf * HALF:(hf + 1) * HALF], slice(hf * HALF, (hf + 1) * HALF)
                act.wait_ge(rope_ready, i + 1)
                nc.scalar.copy(parts[:, w, 0, :, c], src).then_inc(hi_ready, 1)
                act.wait_ge(res_ready, i + 1)
                nc.scalar.copy(parts[:, w, 1, :, c], resid[:, i % 2]).then_inc(mid_ready, 1)
            for i in range(4):
                act.wait_ge(v_ps, i + 1)
                nc.scalar.copy(v[:, 2 * i:2 * i + 2], psum[:, i].rearrange("p (n c) -> p n c", n=2)).then_inc(v_ready, 1)
            for i in range(2):
                act.wait_ge(neg_ready, i + 1)
                nc.scalar.activation(tmp, tmp, ACT.Exp).then_inc(nexp_ready, 1)
            for i in range(4):
                b, g = i // 2, i % 2
                act.wait_ge(kft_ps, i + 1)
                nc.scalar.copy(kfeat_tok[:, 4 * g:4 * g + 4, b * P:(b + 1) * P],
                               psum[:, i].rearrange("p (n c) -> p n c", n=4)).then_inc(kft_ready, 1)

            def quad(qd):
                for t in range(QSTEP):
                    n, g = QSTEP * qd + t, t // 4
                    if t % 4 == 0:
                        act.wait_ge(av_ps, 16 * qd + g - 1 if g else 16 * qd)
                    act.wait_ge(sct_ps, n + 1)
                    nc.scalar.activation(prob[:, t % 8], psum[:, 4 + t % 2], ACT.Exp,
                                         scale=HD ** -0.5).then_inc(exp_ready, 1)
                    if t in (39, 63):
                        hf = t // 63
                        act.wait_ge(av_ps, 16 * qd + 8 * (hf + 1))
                        act.wait_ge(osb_out[hf], 16 * qd)
                        nc.scalar.copy(osb[:, hf], psum[:, 6]).then_inc(osb_ready, 1)

            with act.Fori(0, NQ) as qd:
                quad(qd)
            for i in range(4):
                act.wait_ge(xn2T_ps, i + 1)
                hf, b = i // 2, i % 2
                nc.scalar.copy(xn2T[:, b, hf * HALF:(hf + 1) * HALF], psum[:, 4 + i]).then_inc(xn2T_ready, 1)
            act.wait_ge(top_ready, 1)
            nc.scalar.activation(pw_e, pw_d, ACT.Exp).then_inc(pexp_ready, 1)

            def silu(t, par):
                act.wait_ge(gu_ps, t + 1)
                nc.scalar.activation(act_g[:, par].rearrange("p (b c) -> p b c", b=2),
                                     psum[:, 0:2, 0:FN], ACT.Silu).then_inc(silu_ready, 1)

            def y_copy(t, par):
                act.wait_ge(y_ps, t + 1)
                nc.scalar.copy(yt[:, par], psum[:, 6, 0:H]).then_inc(y_ready, 1)

            silu(0, 0)
            with act.Fori(0, (NTILE - 1) // 2) as i:
                for r in (1, 2):
                    t = 2 * i + r
                    silu(t, r % 2)
                    act.wait_ge(y_out[(r + 1) % 2], 16 * i)
                    y_copy(t - 1, (r + 1) % 2)
            act.wait_ge(y_out[(NTILE - 1) % 2], 16 * ((NTILE - 1) // 2))
            y_copy(NTILE - 1, (NTILE - 1) % 2)

        @block.vector
        def _(dve):
            V = nc.vector
            chain = [0]

            def link(ins):
                chain[0] += 1
                ins.then_inc(dve_step, 1)
                dve.wait_ge(dve_step, chain[0])

            def moments(lo, hi):
                for n in range(lo, hi):
                    ins = V.bn_stats(stat[:, n], x[:, n])
                link(ins)
                for n in range(lo, hi):
                    ins = V.bn_aggr(mv[:, n], stat[:, n])
                link(ins)
                V.tensor_scalar(rstd[:, lo:hi], mv[:, lo:hi, 1], EPS, None, ALU.add).then_inc(var_ready, 1)

            for i in range(4):
                dve.wait_ge(x_in[i], 16)
                moments(2 * i, 2 * i + 2)
            dve.wait_ge(const_in, 16)
            V.tensor_copy(ident_b, ident).then_inc(identb_ready, 1)
            V.tensor_copy(tri_b, const[:, C_TRI:C_TRI + P])
            V.memset(ones_b, 1.0)
            for i in range(4):
                dve.wait_ge(rstd_ready, i + 1)
                for n in (2 * i, 2 * i + 1):
                    V.tensor_scalar(xn[:, n], x[:, n], mv[:, n, 0:1], rstd[:, n:n + 1],
                                    ALU.subtract, ALU.mult).then_inc(xn_ready, 1)
            dve.wait_ge(gexp_ready, 1)
            link(V.tensor_scalar(gate_1, gate_e, 1.0, None, ALU.add))
            link(V.reciprocal(gate, gate_1))
            V.tensor_tensor(omg, gate, gate_e, ALU.mult).then_inc(gate_ready, 1)
            dve.wait_ge(rope_in, 16)

            def split(i):
                w, hf = QK_IDX[i]
                c = slice(hf * HALF, (hf + 1) * HALF)
                src = (kT, qT)[w][:, :, c]
                dve.wait_ge(hi_ready, i + 1)
                V.tensor_tensor(resid[:, i % 2], src, parts[:, w, 0, :, c], ALU.subtract).then_inc(res_ready, 1)
                dve.wait_ge(mid_ready, i + 1)
                V.tensor_tensor(parts[:, w, 2, :, c], resid[:, i % 2], parts[:, w, 1, :, c],
                                ALU.subtract).then_inc(lo_ready, 1)

            for i, (w, hf) in enumerate(QK_IDX):
                c = slice(hf * HALF, (hf + 1) * HALF)
                b = 4 + 2 * (i % 2)
                dve.wait_ge(qk_ps, i + 1)
                if i:
                    dve.wait_ge(rope_ready, i)
                V.tensor_tensor(tmp[:, 0], psum[:, b], rope[:, 0, c], ALU.mult)
                V.tensor_tensor(tmp[:, 1], psum[:, b + 1], rope[:, 1, c], ALU.mult)
                V.tensor_tensor(tmp[:, 2], psum[:, b + 1], rope[:, 0, c], ALU.mult)
                V.tensor_tensor(tmp[:, 3], psum[:, b], rope[:, 1, c], ALU.mult).then_inc(rope_mul, 1)
                if i:
                    split(i - 1)
            split(3)
            tv = tmp.rearrange("p (b h) c -> p b (h c)", b=HB)
            for i, (src, dst) in enumerate(((kT, kfeat), (qT, qfeat))):
                dve.wait_ge(nexp_ready, i + 1)
                if i == 1:
                    dve.wait_ge(v_ps, 4)
                V.scalar_tensor_tensor(out=dst, in0=src, scalar=0.0, in1=tv, op0=ALU.max, op1=ALU.add).then_inc(feat_ready, 1)
            for b in range(HB):
                dve.wait_ge(st_ps, b + 1)
                for k in range(2):
                    ins = V.tensor_tensor(state[:, b, k * P:(k + 1) * P], psum[:, 4 + b, k * P:(k + 1) * P],
                                          const[:, C_MASK:C_MASK + P], ALU.mult)
                ins.then_inc(st_ready, 1)
            for i in range(4):
                b, c = i // 2, slice((i % 2) * HALF, (i % 2 + 1) * HALF)
                dve.wait_ge(lin_ps, i + 1)
                link(V.reciprocal(tmp[:, i], psum[:, 2 * i + 1]))
                V.scalar_tensor_tensor(out=memT[:, b, c], in0=psum[:, 2 * i], scalar=gate[:, b:b + 1],
                                       in1=tmp[:, i], op0=ALU.mult, op1=ALU.mult).then_inc(lin_ready, 1)

            def reduce_max(pairs, s):
                u, k = s // 32, (s % 32) // 2
                dve.wait_ge(sc_ps, pairs + 1)
                V.tensor_reduce(mx[:, u, k:k + 1], banks(2 * (s // 2 % 2), 2), AX.X, ALU.max).then_inc(max_ready, 1)

            def max_parts(unit, u, pairs):
                dve.wait_ge(max_ready, pairs)
                V.tensor_copy(mhl[:, 0], mx[:, u]).then_inc(mhl_ready, 1)
                dve.wait_ge(mhl_ready, 2 * unit + 1)
                V.tensor_tensor(mhl[:, 1], mx[:, u], mhl[:, 0], ALU.subtract).then_inc(mhl_ready, 1)

            def max_turned(unit):
                dve.wait_ge(mT_ps, unit + 1)
                dve.wait_ge(max_out, 16 * unit)
                V.tensor_copy(mT, psum[0:32, 7, 0:P // 2].bitcast(BF16)).then_inc(mT_ready, 1)

            def score_side(qd, nxt, s):
                if s % 2:
                    reduce_max(32 * (qd + nxt) + s // 2, s)
                if s % 32 == 31:
                    max_parts(2 * (qd + nxt) + s // 32, s // 32, 32 * (qd + nxt) + s // 2 + 1)

            for s in range(LEAD):
                score_side(0, 0, s)
                if s == 35:
                    max_turned(0)

            def quad(qd, more):
                for step in score_steps(more):
                    if step is not None:
                        nxt, s = step
                        score_side(qd, nxt, s)
                        if s == 63 and not more:
                            max_turned(2 * qd + 1)
                        if nxt and s == 3:
                            max_turned(2 * qd + 1)
                        if nxt and s == 35:
                            max_turned(2 * qd + 2)

            with dve.Fori(0, NQ - 1) as qd:
                quad(qd, True)
            quad(NQ - 1, False)
            for i in range(4):
                hf, b = i // 2, i % 2
                c = slice(hf * HALF, (hf + 1) * HALF)
                dve.wait_ge(num_in[i], 32)
                link(V.reciprocal(den[:, b, c], den[:, b, c]))
                link(V.scalar_tensor_tensor(out=num[:, b, c], in0=num[:, b, c], scalar=omg[:, b:b + 1],
                                            in1=den[:, b, c], op0=ALU.mult, op1=ALU.mult))
                V.tensor_tensor(num[:, b, c], num[:, b, c], memT[:, b, c], ALU.add).then_inc(mix_ready, 1)
            for i in range(4):
                dve.wait_ge(wo_ps, i + 1)
                link(V.tensor_tensor(x[:, 2 * i:2 * i + 2], x[:, 2 * i:2 * i + 2],
                                     psum[:, i].rearrange("p (n c) -> p n c", n=2), ALU.add))
            moments(0, TT)
            dve.wait_ge(rstd_ready, 5)
            for n in range(TT):
                V.tensor_scalar(xn2[:, n], x[:, n], mv[:, n, 0:1], rstd[:, n:n + 1],
                                ALU.subtract, ALU.mult).then_inc(xn2_ready, 1)
            dve.wait_ge(lg_ps, 1)
            link(V.tensor_copy(lg, psum[:, 0, 0:TT * E].rearrange("p (n e) -> p n e", e=E)))
            for n in range(TT):
                ins = V.max(top[:, n], lg[:, n])
            link(ins)
            V.tensor_tensor(pw_d, top[:, :, 1], top[:, :, 0], ALU.subtract).then_inc(top_ready, 1)
            for n in range(TT):
                ins = V.max_index(topi[:, n], top[:, n], lg[:, n])
            link(ins)
            link(V.tensor_copy(topf, topi[:, :, 0:K]))
            iota = const[:, C_IOTA:C_IOTA + E].unsqueeze(1).to_broadcast([P, TT, E])
            for k in range(K):
                ins = V.tensor_tensor(onehot[:, k], topf[:, :, k:k + 1].to_broadcast([P, TT, E]), iota, ALU.is_equal)
            link(ins)
            V.tensor_tensor(chosen, onehot[:, 0], onehot[:, 1], ALU.add).then_inc(chosen_ready, 1)
            dve.wait_ge(pexp_ready, 1)
            link(V.tensor_scalar(pw_s, pw_e, 1.0, None, ALU.add))
            link(V.reciprocal(pw[:, 0], pw_s))
            V.tensor_tensor(pw[:, 1], pw[:, 0], pw_e, ALU.mult)
            dve.wait_ge(rank_ps, 1)
            link(V.tensor_copy(cnt, psum[:, 1, 0:E]))
            link(V.tensor_tensor(cmp, cnt.unsqueeze(2).to_broadcast([P, E, E]),
                                 const[:, C_J:C_J + E * E].rearrange("p (e j) -> p e j", e=E), ALU.is_gt))
            link(V.tensor_reduce(tiles, cmp, AX.X, ALU.add))
            link(V.tensor_tensor(cmp, tiles.unsqueeze(1).to_broadcast([P, E, E]),
                                 const[:, C_LTI:C_LTI + E * E].rearrange("p (e j) -> p e j", e=E), ALU.mult))
            link(V.tensor_reduce(cum, cmp, AX.X, ALU.add))
            link(V.tensor_tensor(base_t, cum, tiles, ALU.subtract))
            link(V.tensor_scalar(base, base_t, float(P), None, ALU.mult))
            link(V.tensor_tensor(pos, psum[:, 0, 0:TT * E].rearrange("p (n e) -> p n e", e=E),
                                 base.unsqueeze(1).to_broadcast([P, TT, E]), ALU.add))
            for k in range(K):
                ins = V.tensor_tensor(sel[:, k], onehot[:, k], pos, ALU.mult)
            link(ins)
            link(V.tensor_reduce(slot_f, sel, AX.X, ALU.add))
            V.tensor_copy(slot, slot_f).then_inc(slot_ready, 1)
            link(V.tensor_tensor(tau, cum.unsqueeze(1).to_broadcast([P, NTILE + 1, E]),
                                 const[:, C_TAU:].rearrange("p (n e) -> p n e", e=E), ALU.is_le))
            link(V.tensor_reduce(ex_f, tau, AX.X, ALU.add))
            V.tensor_scalar(ex_i, ex_f, float(E - 1), None, ALU.min).then_inc(expert_ready, 1)

            def xgT_copy(t, par):
                dve.wait_ge(xgT_ps, t + 1)
                V.tensor_copy(xgT[:, par], psum[:, 7, 0:HB * P].rearrange("p (b c) -> p b c", b=HB)).then_inc(xgT_ready, 1)

            def hidden(t, par):
                dve.wait_ge(silu_ready, t + 1)
                V.tensor_tensor(hid[:, par].rearrange("p (b c) -> p b c", b=2),
                                act_g[:, par].rearrange("p (b c) -> p b c", b=2),
                                psum[:, 2:4, 0:FN], ALU.mult).then_inc(hid_ready, 1)

            def hidT_copy(t, par):
                dve.wait_ge(hidT_ps, t + 1)
                V.tensor_copy(hidT[:, par, 0:4], psum[:, 4].rearrange("p (c t) -> p c t", c=4))
                V.tensor_copy(hidT[0:FB[4], par, 4:6], psum[0:FB[4], 5, 0:2 * P].rearrange("p (c t) -> p c t", c=2)
                              ).then_inc(hidT_ready, 1)

            xgT_copy(0, 0)
            xgT_copy(1, 1)
            hidden(0, 0)
            hidT_copy(0, 0)
            with dve.Fori(0, (NTILE - 1) // 2) as i:
                for r in (1, 2):
                    t = 2 * i + r
                    xgT_copy(t + 1, (r + 1) % 2)
                    hidden(t, r % 2)
                    hidT_copy(t, r % 2)
            for n in range(TT):
                dve.wait_ge(gath_in[n], 32)
                link(V.scalar_tensor_tensor(out=x[:, n], in0=gath[:, 0, n], scalar=pw[:, 0, n:n + 1],
                                            in1=x[:, n], op0=ALU.mult, op1=ALU.add))
                V.scalar_tensor_tensor(out=x[:, n], in0=gath[:, 1, n], scalar=pw[:, 1, n:n + 1],
                                       in1=x[:, n], op0=ALU.mult, op1=ALU.add).then_inc(out_ready, 1)

        @block.tensor
        def _(pe):
            def mm(*a, **k):
                return nc.tensor.matmul(*a, **k)

            def turn(ready, done, src, bank0):
                for hf in range(2):
                    pe.wait_ge(ready, 4 * hf + 4)
                    for b in range(HB):
                        for n in range(4):
                            ins = nc.tensor.transpose(psum[:, bank0 + 2 * hf + b, n * P:(n + 1) * P],
                                                      src[:, 4 * hf + n, b * P:(b + 1) * P], ident)
                        ins.then_inc(done, 1)

            pe.wait_ge(const_in, 16)
            turn(xn_ready, xnT_ps, xn, 0)
            for i, (w, hf) in enumerate(QK_IDX):
                pe.wait_ge(xnT_ready, 2 * hf + 2)
                pe.wait_ge(w_in[w], 16)
                if i >= 2:
                    pe.wait_ge(rope_mul, i - 1)
                for o in range(HB):
                    for b in range(HB):
                        ins = mm(psum[:, 4 + 2 * (i % 2) + o], wqkv[:, w, b, o * P:(o + 1) * P],
                                 xnT[:, b, hf * HALF:(hf + 1) * HALF], start=(b == 0), stop=(b == HB - 1))
                ins.then_inc(qk_ps, 1)
            pe.wait_ge(w_in[2], 16)
            for n in range(TT):
                for b in range(HB):
                    ins = mm(psum[:, n // 2, (n % 2) * H:(n % 2 + 1) * H], xnT[:, b, n * P:(n + 1) * P],
                             wqkv[:, 2, b], start=(b == 0), stop=(b == HB - 1))
                if n % 2:
                    ins.then_inc(v_ps, 1)
            pe.wait_ge(feat_ready, 1)
            for b in range(HB):
                for g in range(2):
                    pe.wait_ge(v_ready, 2 * b + g + 1)
                    for n in range(4):
                        ins = nc.tensor.transpose(psum[:, 2 * b + g, n * P:(n + 1) * P],
                                                  kfeat[:, b, (4 * g + n) * P:(4 * g + n + 1) * P], ident)
                    ins.then_inc(kft_ps, 1)
            pe.wait_ge(ones_set, 1)
            pe.wait_ge(rope_mul, 4)
            for b in range(HB):
                pe.wait_ge(kft_ready, 2 * b + 2)
                for k in range(2):
                    for n in range(TT):
                        rhs = v[:, n, b * P:(b + 1) * P] if k == 0 else ones
                        ins = mm(psum[:, 4 + b, k * P:(k + 1) * P], kfeat_tok[:, n, b * P:(b + 1) * P], rhs,
                                 start=(n == 0), stop=(n == TT - 1))
                ins.then_inc(st_ps, 1)
            pe.wait_ge(feat_ready, 2)
            pe.wait_ge(st_ready, 2)
            for i in range(4):
                b, c = i // 2, slice((i % 2) * HALF, (i % 2 + 1) * HALF)
                for k in range(2):
                    ins = mm(psum[:, 2 * i + k], state[:, b, k * P:(k + 1) * P], qfeat[:, b, c],
                             start=True, stop=True)
                ins.then_inc(lin_ps, 1)
            pe.wait_ge(lin_ready, 4)
            pe.wait_ge(kst_set, 1)
            pe.wait_ge(identb_ready, 1)

            def score(qd, nxt, s):
                u, k, kh = s // 32, (s % 32) // 2, s % 2
                j, qb = k // 4, k % 4
                pair, sl = 32 * (qd + nxt) + s // 2, (qd + nxt) % 2
                if s == 0:
                    pe.wait_ge(stack_in, 2 * GROUPS * 16 * (qd + nxt + 1))
                if kh == 0 and not (isinstance(pair, int) and pair < 2):
                    pe.wait_ge(max_ready, pair - 1)
                q0 = u * HALF + qb * P
                ins = mm(psum[:, 2 * (s // 2 % 2) + kh], qst[0:SROWS, sl, j, q0:q0 + P],
                         kst[0:SROWS, sl, j, kh * HALF:(kh + 1) * HALF], start=True, stop=True)
                if kh:
                    ins.then_inc(sc_ps, 1)

            def turn_max(unit):
                pe.wait_ge(mhl_ready, 2 * unit + 2)
                nc.tensor.transpose(psum[0:32, 7, 0:P // 2].bitcast(BF16),
                                    mhl.rearrange("p s k -> p (s k)"), ident_b).then_inc(mT_ps, 1)

            def score_t(qd, t):
                u, kb, j = t // 32, (t % 32) // 4, t % 4
                n, sl = QSTEP * qd + t, qd % 2
                if t % 32 == 0:
                    pe.wait_ge(mrow_in, 16 * (2 * qd + u + 1))
                if t >= 2:
                    pe.wait_ge(exp_ready, n - 1)
                mm(psum[:, 4 + t % 2], kst[0:SROWS + 2, sl, j, kb * P:(kb + 1) * P],
                   qst[0:SROWS + 2, sl, j, u * HALF:(u + 1) * HALF], start=True, stop=True).then_inc(sct_ps, 1)

            def product(qd, g):
                u, kb = g // 8, g % 8
                pe.wait_ge(exp_ready, QSTEP * qd + 4 * g + 4)
                if kb == 0:
                    pe.wait_ge(osb_ready, 2 * qd + u)
                    pe.wait_ge(v_staged, qd + 1)
                for j in range(4):
                    ins = mm(psum[32 * j:32 * j + 32, 6], vst[:, kb, j], prob[:, (4 * g + j) % 8],
                             start=(kb == 0), stop=(kb == 7), skip_group_check=True)
                ins.then_inc(av_ps, 1)

            for s in range(LEAD):
                score(0, 0, s)
                if s == 35:
                    turn_max(0)
            pe.wait_ge(vst_set, 1)

            def quad(qd, more):
                held = []
                for t, step in enumerate(score_steps(more)):
                    score_t(qd, t)
                    if step is not None:
                        held.append(step)
                    if t < QSTEP - 4 or t == QSTEP - 1:
                        for nxt, s in held:
                            score(qd, nxt, s)
                            if nxt and s == 3:
                                turn_max(2 * qd + 1)
                            if nxt and s == 35:
                                turn_max(2 * qd + 2)
                        held = []
                    if not more and t == QSTEP - LEAD + 3:
                        turn_max(2 * qd + 1)
                    if t % 4 == 3 and t > 3:
                        product(qd, t // 4 - 1)
                product(qd, QSTEP // 4 - 1)

            with pe.Fori(0, NQ - 1) as qd:
                quad(qd, True)
            quad(NQ - 1, False)

            pe.wait_ge(wo_in, 16)
            for n in range(TT):
                pe.wait_ge(mix_ready, 2 * (n // 4) + 2)
                for b in range(HB):
                    ins = mm(psum[:, n // 2, (n % 2) * H:(n % 2 + 1) * H], num[:, b, n * P:(n + 1) * P],
                             wo[:, b], start=(b == 0), stop=(b == HB - 1))
                if n % 2:
                    ins.then_inc(wo_ps, 1)
            turn(xn2_ready, xn2T_ps, xn2, 4)
            pe.wait_ge(router_in, 16)
            pe.wait_ge(xn2T_ready, 4)
            for n in range(TT):
                for b in range(HB):
                    ins = mm(psum[:, 0, n * E:(n + 1) * E], xn2T[:, b, n * P:(n + 1) * P], router[:, b],
                             start=(b == 0), stop=(b == HB - 1))
            ins.then_inc(lg_ps, 1)
            pe.wait_ge(chosen_ready, 1)
            mm(psum[:, 0, 0:TT * E], tri_b, chosen.rearrange("p n e -> p (n e)"), start=True, stop=False)
            for n in range(TT - 1):
                m = TT - 1 - n
                mm(psum[:, 0, (n + 1) * E:TT * E].rearrange("p (n e) -> p n e", e=E), ones_b,
                   chosen[:, n:n + 1].to_broadcast([P, m, E]), start=False, stop=(n == TT - 2))
            for n in range(TT):
                ins = mm(psum[:, 1, 0:E], ones_b, chosen[:, n], start=(n == 0), stop=(n == TT - 1))
            ins.then_inc(rank_ps, 1)

            def load_expert(t):
                return pe.value_load(ex_i[0:1, bass.ts(t, 1)], min_val=0, max_val=E - 1)

            def gate_up(t, par, e):
                pe.wait_ge(xgT_ready, t + 1)
                if not (isinstance(t, int) and t == 0):
                    pe.wait_ge(hid_ready, t)
                for c in range(4):
                    for b in range(HB):
                        ins = mm(psum[:, c, 0:FN], xgT[:, par, b], gu[:, b, e, c * FN:(c + 1) * FN],
                                 start=(b == 0), stop=(b == HB - 1))
                ins.then_inc(gu_ps, 1)

            def turn_x(t, par):
                pe.wait_ge(xg_in[par], 16 * (t // 2 + 1) if isinstance(t, int) else t)
                for b in range(HB):
                    ins = nc.tensor.transpose(psum[:, 7, b * P:(b + 1) * P], xg[:, par, b * P:(b + 1) * P], ident)
                ins.then_inc(xgT_ps, 1)

            def turn_hidden(t, par):
                pe.wait_ge(hid_ready, t + 1)
                for c, (o, n) in enumerate(zip(FO, FB)):
                    ins = nc.tensor.transpose(psum[0:n, 4 + c // 4, (c % 4) * P:(c % 4 + 1) * P],
                                              hid[:, par, o:o + n], ident)
                ins.then_inc(hidT_ps, 1)

            def down(t, par, e):
                pe.wait_ge(hidT_ready, t + 1)
                pe.wait_ge(y_ready, t)
                for c, n in enumerate(FB):
                    ins = mm(psum[:, 6, 0:H], hidT[0:n, par, c], dn[0:n, c, e], start=(c == 0),
                             stop=(c == len(FB) - 1))
                ins.then_inc(y_ps, 1)

            pe.wait_ge(expert_ready, 1)
            pe.wait_ge(gu_in, 16 * E)
            turn_x(0, 0)
            pe.wait_ge(xgT_ready, 1)
            turn_x(1, 1)
            gate_up(0, 0, load_expert(0))
            turn_hidden(0, 0)
            pe.wait_ge(dn_in, 16 * len(FB))
            with pe.Fori(0, (NTILE - 1) // 2) as i:
                for r in (1, 2):
                    t = 2 * i + r
                    gate_up(t, r % 2, load_expert(t))
                    pe.wait_ge(xg_in[(r + 1) % 2], 16 * (i + 2))
                    for b in range(HB):
                        ins = nc.tensor.transpose(psum[:, 7, b * P:(b + 1) * P],
                                                  xg[:, (r + 1) % 2, b * P:(b + 1) * P], ident)
                    ins.then_inc(xgT_ps, 1)
                    down(t - 1, (r + 1) % 2, load_expert(t - 1))
                    turn_hidden(t, r % 2)
            down(NTILE - 1, (NTILE - 1) % 2, load_expert(NTILE - 1))


def kernel(**inputs):
    from concourse import bacc
    from concourse.bass_utils import run_bass_kernel_spmd

    f = {n.removeprefix("L0_"): np.asarray(a) for n, a in inputs.items()}
    rows = lambda w: w.T.reshape(HB, P, -1).transpose(1, 0, 2)
    weights = np.stack([rows(f[n]) for n in ("attn_Wk", "attn_Wq", "attn_Wv", "attn_Wo")], 1)
    gate_up = np.concatenate([f["ffn_gate_w"], f["ffn_up_w"]], 1)
    const, rope = constants()
    arrays = {
        "x": f["attn_hidden_states"],
        "weights": weights,
        "rope": rope,
        "const": const,
        "gate": np.repeat(f["attn_gate"].reshape(-1), HD).reshape(HB, P).T,
        "router": rows(f["ffn_router_w"]),
        "gate_up": gate_up.transpose(2, 0, 1).reshape(HB, P, E, 2 * F).transpose(1, 0, 2, 3),
        "down": f["ffn_down_w"].transpose(2, 0, 1),
    }
    arrays = {n: np.ascontiguousarray(a) for n, a in arrays.items()}
    nc = bacc.Bacc("TRN2", target_bir_lowering=False, num_devices=1)
    args = [nc.dram_tensor(n, a.shape, mybir.dt.from_np(a.dtype), kind="ExternalInput").ap()
            for n, a in arrays.items()]
    args.append(nc.dram_tensor("out", [1, T, H], F32, kind="ExternalOutput").ap())
    block_kernel(nc, *args)
    return run_bass_kernel_spmd(nc, [arrays], core_ids=[0]).results[0]["out"]
```

```python
from contextlib import ExitStack

import concourse.bass as bass
from concourse import mybir
from concourse.alu_op_type import AluOpType as ALU
import numpy as np

ACT = mybir.ActivationFunctionType
F32, BF16, U32, I32 = mybir.dt.float32, mybir.dt.bfloat16, mybir.dt.uint32, mybir.dt.int32
AX = mybir.AxisListType

P = 128
T, H, NH = 1024, 256, 16
HD = H // NH
TT, HB = T // P, H // P
HALF = T // 2
E, F, K = 8, 688, 2
FB = [P, P, P, P, 88, 88]
FO = [sum(FB[:i]) for i in range(len(FB))]
FN = F // 2
NTILE = (K * T + E * (P - 1)) // P
PAIRS = (NTILE - 1) // 2
NSLOT = (E * T) + P
ROW = H + 2
EPS = 1e-5
NQ = NH // 4
UNITS = 2 * NQ
STEPS = 32
GROUPS = 6
QPART = [0, 0, 1, 1, 0, 2]
KPART = [0, 1, 0, 1, 2, 0]
SROWS = GROUPS * HD
LEAD = 44
PEEL = 11

C_ID, C_MASK, C_TRI, C_LTI, C_J, C_IOTA = 0, 128, 256, 384, 448, 512
C_EVEN = C_IOTA + E
C_ROW0 = C_EVEN + PAIRS
C_PAD = C_ROW0 + NTILE + 1
C_TOK = C_PAD + 1
C_LIST = C_TOK + TT
C_TAU = C_LIST + E
NCONST = C_TAU + (NTILE + 1) * E


def constants():
    c = np.zeros((P, NCONST), np.float32)
    p = np.arange(P)
    c[:, C_ID:C_ID + P] = np.eye(P)
    c[:, C_MASK:C_MASK + P] = p[:, None] // HD == p[None] // HD
    c[:, C_TRI:C_TRI + P] = p[:, None] < p[None]
    e = np.arange(E)
    c[:, C_LTI:C_LTI + E * E] = (e[None] <= e[:, None]).reshape(-1)
    c[:, C_J:C_J + E * E] = np.tile(np.arange(T // P) * P, E)
    c[:, C_IOTA:C_IOTA + E] = e
    c[:, C_EVEN:C_EVEN + PAIRS] = 2 * np.arange(1, PAIRS + 1)
    c[:, C_ROW0:C_ROW0 + NTILE + 1] = P * np.arange(NTILE + 1)
    c[:, C_PAD] = T + p
    c[:, C_TOK:C_TOK + TT] = np.arange(TT) * P + p[:, None]
    c[:, C_LIST:C_LIST + E] = e * T
    c[:, C_TAU:] = np.repeat(np.arange(NTILE + 1), E)
    inv_freq = np.float32(1) / np.float32(10000) ** (np.arange(0, H, 2, dtype=np.float32) / np.float32(H))
    angle = inv_freq[:, None] * np.arange(T, dtype=np.float32)[None]
    return c, np.stack([np.cos(angle), np.sin(angle)], 1).astype(np.float32)


def block_kernel(nc, x_d, w_d, rope_d, const_d, gate_d, router_d, gu_d, dn_d, out_d):
    ctx = ExitStack()
    with ctx:
        WORDS = 53200
        mem = ctx.enter_context(nc.sbuf_tensor("mem", [P, WORDS], F32))
        psum = ctx.enter_context(nc.psum_tensor("psum", [P, 8, 512], F32))

        def words(at, *shape, dt=F32, parts=P):
            n = int(np.prod(shape))
            v = mem[0:parts, at:at + (n if dt != BF16 else n // 2)]
            if dt != F32:
                v = v.bitcast(dt)
            names = "abcd"[:len(shape)]
            if len(shape) > 1:
                v = v.rearrange(f"p ({' '.join(names)}) -> p {' '.join(names)}",
                                **dict(zip(names, shape)))
            return v

        G = 0
        gu = words(G, E, HB, 2 * F)
        xn = words(G, TT, H)
        kfeat_tok = words(G, TT, H)
        xnT = words(G + 2048, HB, T)
        qfeat = words(G + 2048, HB, T)
        rope = words(G + 4096, 2, T)
        relu = words(G + 4096, HB, T)
        wqkv = words(G + 6144, 3, HB, H)
        kT = words(G + 7680, HB, T)
        qT = words(G + 9728, HB, T)
        parts = words(G + 11776, 2, 3, HB, T, dt=BF16)
        tmp = words(G + 17920, 4, HALF)
        kfeat = words(G + 19968, HB, T)
        late = G + (E - 1) * HB * 2 * F
        osb = words(late, 2, HALF)
        combT = words(late + 1024, HB, HALF)
        xn2T = words(late + 1024, HB, HALF)
        A = E * HB * 2 * F
        dn = words(A, len(FB), E, H)
        kst = words(A, NQ, 4, T, dt=BF16)
        qst = words(A + 8192, 4, 4, HALF, dt=BF16)
        prob = words(A + 12288, 8, HALF)
        resid = words(A + 12288, 2, HB, HALF)
        at = [A + 16384]

        def keep(*shape, dt=F32, parts=P):
            n = int(np.prod(shape))
            n = n if dt != BF16 else (n + 1) // 2
            v = words(at[0], *shape, dt=dt, parts=parts)
            at[0] += n
            return v

        x = keep(TT, H)
        b_v = at[0]
        v = keep(TT, HB, P + 8)
        vst = keep(2, TT, 4, 32)
        lin = keep(TT, H)
        b_end = at[0]
        comb = keep(4, H)
        wo = keep(HB, H)
        const = keep(NCONST)
        xn2 = keep(4, K, ROW)
        ident_b = keep(P, dt=BF16)
        state = keep(HB, P + 8)
        stat = keep(TT, 6)
        mv = keep(TT, 2)
        rstd = keep(TT)
        gate = keep(NH)
        gate_e = keep(NH)
        gate_1 = keep(NH)
        omg = keep(NH)
        half_c = keep(TT)
        gate_2 = keep(2, NH)
        lin_r = keep(3, 8)
        lin_g = keep(3, 8)
        den_r = keep(4, 4)
        den_g = keep(4, 4)
        mx = keep(2, 16)
        mhl = keep(2, 16, dt=BF16)
        mT = keep(P, dt=BF16, parts=32)
        router = keep(HB, E)
        lg = keep(4, E)
        top = keep(4, 8)
        topi = keep(4, 8, dt=U32)
        topf = keep(4, K)
        onehot = keep(K, 4, E)
        chosen = keep(TT, E, dt=BF16)
        tri_b = keep(P, dt=BF16)
        ones_b = keep(P, dt=BF16)
        pw_d = keep(4)
        pw_e = keep(4)
        pw_s = keep(4)
        cnt = keep(E)
        cmp = keep(E, E)
        tiles = keep(E)
        cum = keep(E)
        base = keep(E)
        pos = keep(4, E)
        sel = keep(K, 4, E)
        slot_f = keep(K, 4)
        slot = keep(2, K, 4, dt=U32)
        tau = keep(NTILE + 1, E)
        tau_n = keep(NTILE + 1, E)
        ex_f = keep(NTILE + 1)
        ex_n = keep(NTILE + 1)
        ex_r = keep(NTILE + 1)
        ex_i = keep(NTILE + 1, dt=I32)
        row_i = keep(NTILE + 1, dt=I32)
        even = keep(PAIRS)
        pairs_f = keep(1)
        pairs_i = keep(1, dt=I32)
        meta = keep(2, 2, dt=U32)
        meta_y = keep(2, 2, dt=U32)
        assert at[0] <= WORDS, at[0]
        at[0] = b_v
        act_g = keep(2, F)
        hid = keep(2, F)
        hidT = keep(2, len(FB), P)
        xg = keep(2, ROW)
        xgT = keep(2, HB, P)
        yt = keep(2, H)
        assert at[0] <= b_end, at[0] - b_end
        ident = const[:, C_ID:C_ID + P]

        parts_d = nc.dram_tensor("parts_d", [2, 3, H, T], BF16).ap()
        xg_d = nc.dram_tensor("xg_d", [NSLOT, ROW], F32).ap()
        sum_d = nc.dram_tensor("sum_d", [T + P, H], F32).ap()

        def sem(name):
            return ctx.enter_context(nc.semaphore(name))

        x_in = [sem(f"x_in{i}") for i in range(4)]
        w_in = [sem(f"w_in{i}") for i in range(3)]
        rope_in, const_in, gate_in, wo_in, router_in = (sem(n) for n in
            ("rope_in", "const_in", "gate_in", "wo_in", "router_in"))
        ones_set, kst_set, xg_set, xg_filled = (sem(n) for n in ("ones_set", "kst_set", "xg_set", "xg_filled"))
        identb_ready = sem("identb_ready")
        dve_step = sem("dve_step")
        var_ready, rstd_ready, xn_ready, xnT_ps, xnT_ready = (sem(n) for n in
            ("var_ready", "rstd_ready", "xn_ready", "xnT_ps", "xnT_ready"))
        qk_ps, rope_mul, rope_ready = sem("qk_ps"), sem("rope_mul"), sem("rope_ready")
        hi_ready, res_ready, mid_ready, lo_ready = (sem(n) for n in ("hi_ready", "res_ready", "mid_ready", "lo_ready"))
        part_out = [sem(f"part_out{i}") for i in range(4)]
        v_ps, v_ready = sem("v_ps"), sem("v_ready")
        neg_ready, relu_ready, nexp_ready, feat_ready = (sem(n) for n in
            ("neg_ready", "relu_ready", "nexp_ready", "feat_ready"))
        kft_ps, kft_ready, st_ps, st_ready, lin_ps, lin_ready = (sem(n) for n in
            ("kft_ps", "kft_ready", "st_ps", "st_ready", "lin_ps", "lin_ready"))
        gexp_ready, gate_ready = sem("gexp_ready"), sem("gate_ready")
        k_in, q_in = sem("k_in"), sem("q_in")
        k0_in = sem("k0_in")
        sc_ps, max_ready, mhl_ready, mT_ps, mT_ready, mrow_in = (sem(n) for n in
            ("sc_ps", "max_ready", "mhl_ready", "mT_ps", "mT_ready", "mrow_in"))
        sct_ps, exp_ready, av_ps, osb_ready, v_staged = (sem(n) for n in
            ("sct_ps", "exp_ready", "av_ps", "osb_ready", "v_staged"))
        oT_ps, oT_read, mix_ready = sem("oT_ps"), sem("oT_read"), sem("mix_ready")
        combT_ps, combT_ready, wo_ps, x2_ready, xn2_ready, row_ready, xn2T_ps, xn2T_ready = (sem(n) for n in
            ("combT_ps", "combT_ready", "wo_ps", "x2_ready", "xn2_ready", "row_ready", "xn2T_ps", "xn2T_ready"))
        lg_ps, lg_read, top_ready, pexp_ready, chosen_ready, rank_ps, slot_ready, expert_ready = (sem(n) for n in
            ("lg_ps", "lg_read", "top_ready", "pexp_ready", "chosen_ready", "rank_ps", "slot_ready", "expert_ready"))
        sum_init, scattered = sem("sum_init"), sem("scattered")
        gu_in, dn_in = sem("gu_in"), sem("dn_in")
        xg_in = [sem("xg_in0"), sem("xg_in1")]
        xgT_ps, xgT_ready, gu_ps, silu_ready, hid_ready = (sem(n) for n in
            ("xgT_ps", "xgT_ready", "gu_ps", "silu_ready", "hid_ready"))
        hidT_ps, hidT_ready, y_ps, y_ready, y_taken, y_added = (sem(n) for n in
            ("hidT_ps", "hidT_ready", "y_ps", "y_ready", "y_taken", "y_added"))
        out_done = sem("out_done")

        QK_IDX = [(0, 0), (0, 1), (1, 0), (1, 1)]
        x_v = x_d.rearrange("o (n p) h -> p (o n) h", p=P)
        pv = parts_d.rearrange("w s (b p) t -> w s p b t", p=P)
        xg_rows = xg_d.rearrange("(n p) h -> n p h", p=P)
        banks = lambda i, n: psum[:, i:i + n, :].rearrange("p b c -> p (b c)")
        cols = lambda hf: slice(hf * HALF, (hf + 1) * HALF)
        ALL = STEPS * UNITS

        def attention(eng, steps):
            for t in range(PEEL):
                steps(0, t)
            with eng.Fori(0, NQ // 2) as i:
                for t in range(PEEL, 2 * STEPS + PEEL):
                    steps(i, t)
            for t in range(PEEL, NQ * STEPS):
                steps(NQ // 2, t)

        LW = P + 8
        LIN = [list(range(g, min(g + 3, HB * TT))) for g in range(0, HB * TT, 3)]
        LIN_BANK = [4, 5, 6, 7, 6, 7]

        def bank(hf, idx):
            return idx if hf else 7

        POST = {NQ * STEPS + n: w for n, w in {
            13: ("combT", 0), 14: ("copy", 0), 15: ("combT", 1), 16: ("copy", 1),
            18: ("wo", 0), 19: ("add", 0), 27: ("wo", 1), 28: ("add", 1), 31: ("norm", 0),
            STEPS + 12: ("xn2T", 2), STEPS + 13: ("copy", 2), STEPS + 14: ("xn2T", 3),
            STEPS + 15: ("copy", 3), STEPS + 17: ("logits", 0), STEPS + 18: ("choose", 0),
            STEPS + 20: ("top", 0), STEPS + 28: ("rank", 0), STEPS + 29: ("place", 0)}.items()}

        def place(i, t):
            return 2 * i + t // STEPS, t % STEPS, 2 * STEPS * i + t

        block = ctx.enter_context(nc.Block())

        @block.sync
        def _(sp):
            for i in range(4):
                sp.dma_start(x[:, 2 * i:2 * i + 2, :], x_v[:, 2 * i:2 * i + 2, :]).then_inc(x_in[i], 16)
                if i == 1:
                    sp.dma_start(const, const_d).then_inc(const_in, 16)
            sp.dma_start(wqkv[:, 1], w_d[:, 1]).then_inc(w_in[1], 16)
            sp.dma_start(wo, w_d[:, 3]).then_inc(wo_in, 16)
            sp.dma_start(router, router_d).then_inc(router_in, 16)

            def parts_out(i):
                w, hf = QK_IDX[i]
                for s, ready in enumerate((hi_ready, mid_ready, lo_ready)):
                    sp.wait_ge(ready, i + 1)
                    sp.dma_start(pv[w, s][:, :, cols(hf)], parts[:, w, s, :, cols(hf)]).then_inc(part_out[i], 16)

            def k_stack(qd, done):
                for g in range(GROUPS):
                    src = parts_d[0, KPART[g]].rearrange("(q j r) t -> q r j t", j=4, r=HD)[qd]
                    sp.dma_start(kst[g * HD:(g + 1) * HD, qd], src).then_inc(done, 16)

            def q_stack(qd, hf, sl):
                for g in range(GROUPS):
                    src = parts_d[1, QPART[g]].rearrange("(q j r) t -> q r j t", j=4, r=HD)[qd]
                    sp.dma_start(qst[g * HD:(g + 1) * HD, sl], src[:, :, cols(hf)]).then_inc(q_in, 16)

            def max_rows(u, sl):
                sp.wait_ge(mT_ready, u + 1)
                for s in range(2):
                    dst = qst[SROWS + s:SROWS + s + 1, sl].rearrange("p j q -> p (j q)")
                    sp.dma_start(dst, mT[16 * s:16 * s + 16]).then_inc(mrow_in, 16)

            for i in range(3):
                parts_out(i)
            for i in range(2):
                sp.wait_ge(part_out[i], 48)
            k_stack(0, k0_in)
            sp.wait_ge(part_out[2], 48)
            q_stack(0, 0, 0)
            for qd in range(1, NQ):
                k_stack(qd, k_in)
                sp.wait_ge(k_in, 16 * GROUPS * qd)
                sp.wait_ge(q_in, 16 * GROUPS * qd)
                q_stack(qd, 0, qd)
            parts_out(3)
            sp.wait_ge(part_out[3], 48)
            max_rows(0, 0)
            max_rows(1, 1)
            with sp.Fori(1, NQ + 1) as u:
                sp.wait_ge(exp_ready, STEPS * u)
                sp.wait_ge(q_in, 16 * GROUPS * (u + 3))
                q_stack(u - 1, 1, (u + 3) % 4)
                max_rows(u + 1, (u + 1) % 4)
            max_rows(6, 2)
            max_rows(7, 3)

            for hf in range(2):
                sp.wait_ge(x2_ready, 2 * hf + 2)
                sp.dma_start(sum_d[hf * HALF:(hf + 1) * HALF].rearrange("(n p) h -> p n h", p=P),
                             x[:, 4 * hf:4 * hf + 4]).then_inc(sum_init, 16)
            sp.dma_start(sum_d[T:], x[:, 0]).then_inc(sum_init, 16)
            sp.wait_ge(scattered, 16 * K * TT)
            sp.wait_ge(expert_ready, 2)

            def load_xg(t, par):
                row = sp.value_load(row_i[0:1, bass.ts(t, 1)], min_val=0, max_val=E * T)
                sp.dma_start(xg[:, par], xg_d[bass.ds(row, P), :]).then_inc(xg_in[par], 16)

            load_xg(0, 0)
            load_xg(1, 1)
            pairs = sp.value_load(pairs_i[0:1, 0:1], min_val=1, max_val=PAIRS)
            with sp.Fori(0, PAIRS) as i:
                with sp.If_lt(sp.to_reg(i), pairs):
                    for r in (1, 2):
                        t = 2 * i + r
                        sp.wait_ge(xgT_ready, t)
                        load_xg(t + 1, (r + 1) % 2)
            sp.wait_ge(y_added, 32 * pairs + 16)
            sp.dma_start(out_d.rearrange("o (p n) h -> p (o n h)", p=P),
                         sum_d[0:T].rearrange("(p n) h -> p (n h)", p=P)).then_inc(out_done, 16)
            sp.wait_ge(out_done, 16)

        @block.gpsimd
        def _(pool):
            pool.memset(half_c, -0.5).then_inc(ones_set, 1)
            pool.memset(v[:, :, :, P:].rearrange("p n b c -> p (n b) c"), 1.0).then_inc(ones_set, 1)
            pool.memset(vst.rearrange("p a n j c -> p (a n j c)"), 1.0).then_inc(ones_set, 1)
            pool.wait_ge(ones_set, 3)

            def reciprocal_root(c, n):
                pool.wait_ge(var_ready, n)
                nc.gpsimd.tensor_tensor(rstd[:, c], rstd[:, c], half_c[:, c], ALU.pow).then_inc(rstd_ready, 1)

            for g in range(4):
                reciprocal_root(slice(2 * g, 2 * g + 2), g + 1)
            for i, (w, hf) in enumerate(QK_IDX):
                o, c = (kT, qT)[w], cols(hf)
                pool.wait_ge(rope_mul, i + 1)
                nc.gpsimd.tensor_tensor(o[:, 0, c], tmp[:, 0], tmp[:, 1], ALU.subtract)
                nc.gpsimd.tensor_tensor(o[:, 1, c], tmp[:, 2], tmp[:, 3], ALU.add).then_inc(rope_ready, 1)
            tv = tmp.rearrange("p (b h) c -> p b (h c)", b=HB)
            for i, dst in enumerate((kfeat, qfeat)):
                pool.wait_ge(relu_ready, i + 1)
                pool.wait_ge(nexp_ready, i + 1)
                if i == 1:
                    pool.wait_ge(v_ps, 4)
                nc.gpsimd.tensor_tensor(dst, relu, tv, ALU.add).then_inc(feat_ready, 1)

            def stage_v(u, sl, qd):
                c = qd % 2 * 4 * HD
                src = v[:, :, qd // 2, c:c + 4 * HD].rearrange("p n (j c) -> p n j c", c=HD)
                nc.gpsimd.tensor_copy(vst[:, sl, :, :, 0:HD], src).then_inc(v_staged, 1)

            pool.wait_ge(v_ready, 4)
            stage_v(0, 0, 0)
            stage_v(1, 1, 1)
            pool.wait_ge(xg_set, 1)
            pool.wait_ge(lin_ps, len(LIN))
            for i in range(4):
                pool.wait_ge(part_out[i], 48)

            def fill(lo, hi):
                pool.dma_start(xg_d[lo:hi].rearrange("(n p) h -> p n h", p=P),
                               xn2[:, 0, 0:1].to_broadcast([P, (hi - lo) // P, ROW])).then_inc(xg_filled, 16)

            for e in range(E):
                for m in range(2):
                    pool.wait_ge(av_ps, 4 * (e - e % 2) + 2 * (e % 2) + m + 1)
                    if m == 0:
                        fill(e * T, (e + 1) * T)
                    elif e < E - 1:
                        pool.dma_start(gu[:, e], gu_d[:, e]).then_inc(gu_in, 16)
                    else:
                        fill(E * T, NSLOT)
                if e in (2, 4, 6):
                    u = e // 2 + 1
                    stage_v(u, u % 2, u % NQ)
            pool.wait_ge(av_ps, 8 * NQ)
            stage_v(NQ + 1, (NQ + 1) % 2, 1)

            def scatter(hf):
                pool.wait_ge(slot_ready, hf + 1)
                for n in range(4):
                    for k in range(K):
                        pool.indirect_dma_start(
                            out=xg_d, out_offset=bass.IndirectOffsetOnAxis(ap=slot[:, hf, k, n:n + 1], axis=0),
                            in_=xn2[:, n, k], in_offset=None).then_inc(scattered, 16)

            reciprocal_root(slice(0, 4), 5)
            for u in (UNITS - 2, UNITS - 1):
                pool.wait_ge(av_ps, 8 * (u - 1))
                stage_v(u, u % 2, u % NQ)
            pool.wait_ge(xg_filled, 16 * (E + 1))
            scatter(0)
            pool.wait_ge(sct_ps, ALL)
            for c, (o, n) in enumerate(zip(FO, FB)):
                pool.dma_start(dn[0:n, c], dn_d[o:o + n]).then_inc(dn_in, 16)
            reciprocal_root(slice(4, 8), 6)
            scatter(1)
            pool.dma_start(gu[:, E - 1], gu_d[:, E - 1]).then_inc(gu_in, 16)

            pool.wait_ge(sum_init, 48)
            def add_y(t, par):
                pool.wait_ge(y_ready, t + 1)
                pool.sem_inc(y_taken, 1)
                pool.indirect_dma_start(
                    out=sum_d, out_offset=bass.IndirectOffsetOnAxis(ap=meta_y[:, par, 1:2], axis=0),
                    in_=yt[:, par], in_offset=None, compute_op=ALU.add).then_inc(y_added, 16)
                pool.wait_ge(y_added, 16 * t + 16)

            pool.wait_ge(expert_ready, 2)
            pairs = pool.value_load(pairs_i[0:1, 0:1], min_val=1, max_val=PAIRS)
            with pool.Fori(0, PAIRS) as i:
                with pool.If_lt(pool.to_reg(i), pairs):
                    for r in (0, 1):
                        add_y(2 * i + r, r)
            add_y(2 * pairs, 0)

        @block.scalar
        def _(act):
            act.dma_start(wqkv[:, 0], w_d[:, 0]).then_inc(w_in[0], 16)
            act.dma_start(rope, rope_d).then_inc(rope_in, 16)
            act.dma_start(gate, gate_d.to_broadcast([P, NH])).then_inc(gate_in, 16)
            act.dma_start(wqkv[:, 2], w_d[:, 2]).then_inc(w_in[2], 16)
            act.wait_ge(gate_in, 16)
            nc.scalar.activation(gate_e, gate, ACT.Exp, scale=-1.0).then_inc(gexp_ready, 1)
            for hf in range(2):
                for b in range(HB):
                    act.wait_ge(xnT_ps, 2 * hf + b + 1)
                    nc.scalar.copy(xnT[:, b, cols(hf)], psum[:, 2 * hf + b]).then_inc(xnT_ready, 1)
            for i, (w, hf) in enumerate(QK_IDX):
                act.wait_ge(rope_ready, i + 1)
                nc.scalar.copy(parts[:, w, 0, :, cols(hf)], (kT, qT)[w][:, :, cols(hf)]).then_inc(hi_ready, 1)
                if i == 2:
                    act.wait_ge(v_ps, 2)
                    for j in range(2):
                        nc.scalar.copy(v[:, 2 * j:2 * j + 2, :, 0:P],
                                       psum[:, j].rearrange("p (n b c) -> p n b c", n=2, b=HB)).then_inc(v_ready, 1)
                act.wait_ge(res_ready, i + 1)
                nc.scalar.copy(parts[:, w, 1, :, cols(hf)], resid[:, i % 2]).then_inc(mid_ready, 1)
                if i == 2:
                    act.wait_ge(v_ps, 4)
                    for j in range(2, 4):
                        nc.scalar.copy(v[:, 2 * j:2 * j + 2, :, 0:P],
                                       psum[:, j].rearrange("p (n b c) -> p n b c", n=2, b=HB)).then_inc(v_ready, 1)
            for i in range(2):
                act.wait_ge(rope_mul, 4) if i == 0 else act.wait_ge(feat_ready, 1)
                nc.scalar.activation(relu, (kT, qT)[i], ACT.Relu).then_inc(relu_ready, 1)
                act.wait_ge(neg_ready, i + 1)
                nc.scalar.activation(tmp, tmp, ACT.Exp).then_inc(nexp_ready, 1)
            for i in range(4):
                b, g = i // 2, i % 2
                act.wait_ge(kft_ps, i + 1)
                nc.scalar.copy(kfeat_tok[:, 4 * g:4 * g + 4, b * P:(b + 1) * P],
                               psum[:, 4 + i].rearrange("p (n c) -> p n c", n=4)).then_inc(kft_ready, 1)

            def turned_copy(hf, n):
                if n < 2:
                    act.wait_ge(combT_ps, 2 * hf + n + 1)
                    nc.scalar.copy(combT[:, n], psum[:, bank(hf, n)]).then_inc(combT_ready, 1)
                else:
                    act.wait_ge(xn2T_ps, 2 * hf + n - 1)
                    nc.scalar.copy(xn2T[:, n - 2], psum[:, bank(hf, n + 2)]).then_inc(xn2T_ready, 1)

            def second_exp(hf):
                act.wait_ge(top_ready, hf + 1)
                nc.scalar.activation(pw_e, pw_d, ACT.Exp).then_inc(pexp_ready, 1)

            def osb_copy(u, par):
                act.wait_ge(av_ps, 8 * u + 8)
                nc.scalar.copy(osb[:, par], psum[:, 6]).then_inc(osb_ready, 1)

            def steps(i, t):
                u, r, n = place(i, t)
                if t % 4 == 0 and t >= 8:
                    act.wait_ge(av_ps, 16 * i + t // 4 - 1)
                act.wait_ge(sct_ps, n + 1)
                nc.scalar.activation(prob[:, t % 8], psum[:, 4 + t % 2], ACT.Exp,
                                     scale=HD ** -0.5).then_inc(exp_ready, 1)
                if r == 3 and t > 3:
                    osb_copy(u - 1, (t // STEPS - 1) % 2)
                if isinstance(n, int) and n in POST:
                    f, k = POST[n]
                    if f == "copy":
                        turned_copy(0, k)
                    if f == "top":
                        second_exp(0)

            attention(act, steps)
            osb_copy(7, 1)
            turned_copy(1, 0)
            turned_copy(1, 1)
            turned_copy(1, 2)
            turned_copy(1, 3)
            second_exp(1)

            def silu(t, par):
                act.wait_ge(gu_ps, t + 1)
                nc.scalar.activation(act_g[:, par].rearrange("p (b c) -> p b c", b=2),
                                     psum[:, 0:2, 0:FN], ACT.Silu).then_inc(silu_ready, 1)

            def weigh(t, par):
                act.wait_ge(y_ps, t + 1)
                nc.scalar.activation(yt[:, par], psum[:, 6, 0:H], ACT.Copy,
                                     scale=meta_y[:, par, 0:1].bitcast(F32)).then_inc(y_ready, 1)

            act.wait_ge(expert_ready, 2)
            pairs = act.value_load(pairs_i[0:1, 0:1], min_val=1, max_val=PAIRS)
            silu(0, 0)
            with act.Fori(0, PAIRS) as i:
                with act.If_lt(act.to_reg(i), pairs):
                    for r in (1, 2):
                        t = 2 * i + r
                        silu(t, r % 2)
                        act.wait_ge(y_added, 32 * i)
                        weigh(t - 1, (r + 1) % 2)
            act.wait_ge(y_added, 32 * pairs)
            weigh(2 * pairs, 0)

        @block.vector
        def _(dve):
            V = nc.vector
            chain = [0]

            def link(ins):
                chain[0] += 1
                ins.then_inc(dve_step, 1)
                dve.wait_ge(dve_step, chain[0])

            def moments(lo, hi):
                for n in range(lo, hi):
                    ins = V.bn_stats(stat[:, n], x[:, n])
                link(ins)
                for n in range(lo, hi):
                    ins = V.bn_aggr(mv[:, n], stat[:, n])
                link(ins)
                V.tensor_scalar(rstd[:, lo:hi], mv[:, lo:hi, 1], EPS, None, ALU.add).then_inc(var_ready, 1)

            def normalise(i):
                dve.wait_ge(rstd_ready, i + 1)
                for n in (2 * i, 2 * i + 1):
                    V.tensor_scalar(xn[:, n], x[:, n], mv[:, n, 0:1], rstd[:, n:n + 1],
                                    ALU.subtract, ALU.mult).then_inc(xn_ready, 1)

            two = float(np.array(0xBF80BF80, np.uint32).view(np.float32))
            V.memset(mem[SROWS:SROWS + 2, A:A + 2 * NQ * T], two).then_inc(kst_set, 1)
            for i in range(4):
                dve.wait_ge(x_in[i], 16)
                moments(2 * i, 2 * i + 2)
                if i:
                    normalise(i - 1)
            normalise(3)
            dve.wait_ge(const_in, 16)
            V.tensor_copy(ident_b, ident).then_inc(identb_ready, 1)
            V.tensor_copy(tri_b, const[:, C_TRI:C_TRI + P])
            V.memset(ones_b, 1.0)
            V.memset(xn2[:, 0, 0, 0:H + 1], 0.0)
            V.tensor_copy(xn2[:, 0, 0, H + 1:ROW].bitcast(U32), const[:, C_PAD:C_PAD + 1]).then_inc(xg_set, 1)
            dve.wait_ge(gexp_ready, 1)
            link(V.tensor_scalar(gate_1, gate_e, 1.0, None, ALU.add))
            link(V.reciprocal(gate, gate_1))
            for k in range(2):
                V.tensor_copy(gate_2[:, k], gate)
            link(V.tensor_tensor(omg, gate, gate_e, ALU.mult))
            dve.wait_ge(rope_in, 16)

            def split(i):
                w, hf = QK_IDX[i]
                dve.wait_ge(hi_ready, i + 1)
                V.tensor_tensor(resid[:, i % 2], (kT, qT)[w][:, :, cols(hf)], parts[:, w, 0, :, cols(hf)],
                                ALU.subtract).then_inc(res_ready, 1)
                dve.wait_ge(mid_ready, i + 1)
                V.tensor_tensor(parts[:, w, 2, :, cols(hf)], resid[:, i % 2], parts[:, w, 1, :, cols(hf)],
                                ALU.subtract).then_inc(lo_ready, 1)

            for i, (w, hf) in enumerate(QK_IDX):
                c, b = cols(hf), 4 + 2 * (i % 2)
                dve.wait_ge(qk_ps, i + 1)
                if i:
                    dve.wait_ge(rope_ready, i)
                V.tensor_tensor(tmp[:, 0], psum[:, b], rope[:, 0, c], ALU.mult)
                V.tensor_tensor(tmp[:, 1], psum[:, b + 1], rope[:, 1, c], ALU.mult)
                V.tensor_tensor(tmp[:, 2], psum[:, b + 1], rope[:, 0, c], ALU.mult)
                V.tensor_tensor(tmp[:, 3], psum[:, b], rope[:, 1, c], ALU.mult).then_inc(rope_mul, 1)
                if i:
                    split(i - 1)
            split(3)

            def score_side(i, t):
                u, s, _ = place(i, t)
                par, k, pair = t // STEPS % 2, s // 2, STEPS * i + t // 2
                if s % 2:
                    dve.wait_ge(sc_ps, pair + 1)
                    V.tensor_reduce(mx[:, par, k:k + 1], banks(2 * (k % 2), 2), AX.X, ALU.max).then_inc(max_ready, 1)
                if s == STEPS - 1:
                    dve.wait_ge(max_ready, pair + 1)
                    V.tensor_copy(mhl[:, 0], mx[:, par]).then_inc(mhl_ready, 1)
                    dve.wait_ge(mhl_ready, 2 * u + 1)
                    V.tensor_tensor(mhl[:, 1], mx[:, par], mhl[:, 0], ALU.subtract).then_inc(mhl_ready, 1)
                if s == 5 and t > 5:
                    max_turned(u - 1)

            def max_turned(u):
                dve.wait_ge(mT_ps, u + 1)
                dve.wait_ge(mrow_in, 32 * u)
                V.tensor_copy(mT, psum[0:32, 7, 0:P // 2].bitcast(BF16)).then_inc(mT_ready, 1)

            tv = tmp.rearrange("p (b h) c -> p b (h c)", b=HB)

            def minimum(i):
                dve.wait_ge(rope_ready, 4)
                if i == 1:
                    dve.wait_ge(feat_ready, 1)
                V.tensor_scalar(tv, (kT, qT)[i], 0.0, None, ALU.min).then_inc(neg_ready, 1)

            def mask_state():
                dve.wait_ge(st_ps, 2)
                src = psum[:, 4, 0:HB * LW].rearrange("p (b c) -> p b c", b=HB)
                mask = const[:, C_MASK:C_MASK + P]
                V.tensor_tensor(state[:, :, 0:P], src[:, :, 0:P], mask.unsqueeze(1).to_broadcast([P, HB, P]), ALU.mult)
                V.tensor_tensor(state[:, :, P:], src[:, :, P:], mask[:, 0:P:HD].unsqueeze(1).to_broadcast([P, HB, 8]),
                                ALU.mult).then_inc(st_ready, 1)

            def lin_scale(j):
                g0, m = LIN[j][0], len(LIN[j])
                dve.wait_ge(lin_ps, j + 1)
                src = psum[:, LIN_BANK[j], 0:m * LW].rearrange("p (g c) -> p g c", g=m)
                link(V.reciprocal(lin_r[:, 0:m], src[:, :, P:]))
                g = gate_2.rearrange("p a (b h) -> p (a b) h", h=8)[:, g0 % HB:g0 % HB + m]
                link(V.tensor_tensor(lin_g[:, 0:m], lin_r[:, 0:m], g, ALU.mult))
                V.tensor_tensor(lin.rearrange("p n (b h c) -> p (n b) h c", b=HB, c=HD)[:, g0:g0 + m],
                                src[:, :, 0:P].rearrange("p g (h c) -> p g h c", c=HD),
                                lin_g[:, 0:m].unsqueeze(3).to_broadcast([P, m, 8, HD]), ALU.mult).then_inc(lin_ready, 1)

            minimum(0)
            for s in range(LEAD):
                score_side(0, s)
                if s == 7:
                    minimum(1)
                if s == 35:
                    mask_state()
                if s in (41, 43):
                    lin_scale(s // 2 - 20)
            lin_scale(2)
            lin_scale(3)

            def mix(u, qd, hf):
                o = psum[:, 7].rearrange("p (b j c) -> p b j c", b=4, j=4)
                dve.wait_ge(oT_ps, u + 1)
                V.reciprocal(den_r, o[:, :, :, HD]).then_inc(oT_read, 1)
                dve.wait_ge(oT_read, 4 * u + 1)
                om = omg.rearrange("p (q j) -> p q j", q=NQ)[:, qd]
                V.tensor_tensor(den_g, den_r, om.unsqueeze(1).to_broadcast([P, 4, 4]), ALU.mult).then_inc(oT_read, 1)
                dve.wait_ge(oT_read, 4 * u + 2)
                dst = comb.rearrange("p n (q c) -> p q n c", q=NQ)[:, qd]
                V.tensor_tensor(dst.rearrange("p n (j c) -> p n j c", c=HD), o[:, :, :, 0:HD],
                                den_g.unsqueeze(3).to_broadcast([P, 4, 4, HD]), ALU.mult).then_inc(oT_read, 1)
                dve.wait_ge(oT_read, 4 * u + 3)
                src = lin[:, 4 * hf:4 * hf + 4].rearrange("p n (q c) -> p q n c", q=NQ)[:, qd]
                V.tensor_tensor(dst, dst, src, ALU.add).then_inc(oT_read, 1)

            def add_x(hf, n):
                dve.wait_ge(wo_ps, 2 * hf + n + 1)
                c = slice(4 * hf + 2 * n, 4 * hf + 2 * n + 2)
                V.tensor_tensor(x[:, c], x[:, c], psum[:, bank(hf, 2 + n)].rearrange("p (n c) -> p n c", n=2),
                                ALU.add).then_inc(x2_ready, 1)
                dve.wait_ge(x2_ready, 2 * hf + n + 1)

            def second_norm(hf):
                dve.wait_ge(rstd_ready, 5 + hf)
                if hf:
                    dve.wait_ge(scattered, 16 * K * 4)
                else:
                    dve.wait_ge(xg_filled, 16 * (E + 1))
                for n in range(4):
                    m = 4 * hf + n
                    for k in range(K):
                        V.tensor_scalar(xn2[:, n, k, 0:H], x[:, m], mv[:, m, 0:1], rstd[:, m:m + 1],
                                        ALU.subtract, ALU.mult).then_inc(xn2_ready, 1)

            def choose(hf):
                dve.wait_ge(lg_ps, hf + 1)
                V.tensor_copy(lg, psum[:, bank(hf, 6), 0:4 * E].rearrange("p (n e) -> p n e", e=E)).then_inc(lg_read, 1)
                dve.wait_ge(lg_read, hf + 1)
                for n in range(4):
                    ins = V.max(top[:, n], lg[:, n])
                link(ins)
                V.tensor_tensor(pw_d, top[:, :, 1], top[:, :, 0], ALU.subtract).then_inc(top_ready, 1)
                for n in range(4):
                    ins = V.max_index(topi[:, n], top[:, n], lg[:, n])
                link(ins)
                link(V.tensor_copy(topf, topi[:, :, 0:K]))
                iota = const[:, C_IOTA:C_IOTA + E].unsqueeze(1).to_broadcast([P, 4, E])
                for k in range(K):
                    ins = V.tensor_tensor(onehot[:, k], topf[:, :, k:k + 1].to_broadcast([P, 4, E]), iota, ALU.is_equal)
                link(ins)
                V.tensor_tensor(chosen[:, 4 * hf:4 * hf + 4], onehot[:, 0], onehot[:, 1], ALU.add).then_inc(chosen_ready, 1)

            def place_rows(hf):
                dve.wait_ge(pexp_ready, hf + 1)
                link(V.tensor_scalar(pw_s, pw_e, 1.0, None, ALU.add))
                link(V.reciprocal(xn2[:, :, 0, H], pw_s))
                V.tensor_tensor(xn2[:, :, 1, H], xn2[:, :, 0, H], pw_e, ALU.mult)
                for k in range(K):
                    V.tensor_copy(xn2[:, :, k, H + 1].bitcast(U32), const[:, C_TOK + 4 * hf:C_TOK + 4 * hf + 4])
                dve.wait_ge(rank_ps, hf + 1)
                link(V.tensor_tensor(pos, psum[:, bank(hf, 7), 0:4 * E].rearrange("p (n e) -> p n e", e=E),
                                     const[:, C_LIST:C_LIST + E].unsqueeze(1).to_broadcast([P, 4, E]), ALU.add))
                for k in range(K):
                    ins = V.tensor_tensor(sel[:, k], onehot[:, k], pos, ALU.mult)
                link(ins)
                link(V.tensor_reduce(slot_f, sel, AX.X, ALU.add))
                V.tensor_copy(slot[:, hf], slot_f).then_inc(slot_ready, 1)

            def steps(i, t):
                u, r, n = place(i, t)
                if t in (2, 4):
                    lin_scale(3 + t // 2)
                if not (isinstance(n, int) and n + LEAD >= ALL):
                    score_side(i, t + LEAD)
                elif n + LEAD == ALL + 5:
                    max_turned(UNITS - 1)
                if r == 10 and t > 10:
                    unit = u - 1
                    mix(unit, (u + 3) % NQ, 0 if not isinstance(n, int) or unit < NQ else 1)
                if isinstance(n, int) and n in POST:
                    f, k = POST[n]
                    if f == "add":
                        add_x(0, k)
                        if k == 1:
                            moments(0, 4)
                    if f == "norm":
                        second_norm(0)
                    if f == "choose":
                        choose(0)
                    if f == "place":
                        place_rows(0)

            attention(dve, steps)
            mix(UNITS - 1, NQ - 1, 1)
            add_x(1, 0)
            add_x(1, 1)
            moments(4, 8)
            second_norm(1)
            choose(1)
            place_rows(1)

            link(V.tensor_copy(cnt, psum[:, 5, 0:E]))
            link(V.tensor_tensor(cmp, cnt.unsqueeze(2).to_broadcast([P, E, E]),
                                 const[:, C_J:C_J + E * E].rearrange("p (e j) -> p e j", e=E), ALU.is_gt))
            link(V.tensor_reduce(tiles, cmp, AX.X, ALU.add))
            link(V.tensor_tensor(cmp, tiles.unsqueeze(1).to_broadcast([P, E, E]),
                                 const[:, C_LTI:C_LTI + E * E].rearrange("p (e j) -> p e j", e=E), ALU.mult))
            link(V.tensor_reduce(cum, cmp, AX.X, ALU.add))
            link(V.tensor_tensor(even, cum[:, E - 1:E].to_broadcast([P, PAIRS]), const[:, C_EVEN:C_EVEN + PAIRS], ALU.is_ge))
            link(V.tensor_reduce(pairs_f, even, AX.X, ALU.add))
            V.tensor_copy(pairs_i, pairs_f)
            link(V.tensor_tensor(tau, cum.unsqueeze(1).to_broadcast([P, NTILE + 1, E]),
                                 const[:, C_TAU:].rearrange("p (n e) -> p n e", e=E), ALU.is_le))
            V.tensor_reduce(ex_f, tau, AX.X, ALU.add)
            link(V.tensor_tensor(tau_n, tau, tiles.unsqueeze(1).to_broadcast([P, NTILE + 1, E]), ALU.mult))
            link(V.tensor_reduce(ex_n, tau_n, AX.X, ALU.add))
            V.tensor_scalar(ex_i, ex_f, float(E - 1), None, ALU.min).then_inc(expert_ready, 1)
            link(V.scalar_tensor_tensor(out=ex_r, in0=ex_n, scalar=-float(P), in1=const[:, C_ROW0:C_ROW0 + NTILE + 1],
                                        op0=ALU.mult, op1=ALU.add))
            link(V.scalar_tensor_tensor(out=ex_n, in0=ex_f, scalar=float(T), in1=ex_r, op0=ALU.mult, op1=ALU.add))
            V.tensor_scalar(row_i, ex_n, float(E * T), None, ALU.min).then_inc(expert_ready, 1)

            def xgT_copy(t, par):
                dve.wait_ge(xgT_ps, t + 1)
                V.tensor_copy(meta[:, par], xg[:, par, H:ROW].bitcast(U32))
                V.tensor_copy(xgT[:, par], psum[:, 7, 0:HB * P].rearrange("p (b c) -> p b c", b=HB)).then_inc(xgT_ready, 1)

            def hidden(t, par):
                dve.wait_ge(silu_ready, t + 1)
                V.tensor_tensor(hid[:, par].rearrange("p (b c) -> p b c", b=2),
                                act_g[:, par].rearrange("p (b c) -> p b c", b=2),
                                psum[:, 2:4, 0:FN], ALU.mult).then_inc(hid_ready, 1)

            def hidT_copy(t, par):
                dve.wait_ge(hidT_ps, t + 1)
                V.tensor_copy(hidT[:, par, 0:4], psum[:, 4].rearrange("p (c t) -> p c t", c=4))
                V.tensor_copy(hidT[0:FB[4], par, 4:6], psum[0:FB[4], 5, 0:2 * P].rearrange("p (c t) -> p c t", c=2)
                              ).then_inc(hidT_ready, 1)

            dve.wait_ge(expert_ready, 2)
            pairs = dve.value_load(pairs_i[0:1, 0:1], min_val=1, max_val=PAIRS)
            xgT_copy(0, 0)
            dve.wait_ge(xgT_ready, 1)
            V.tensor_copy(meta_y[:, 0], meta[:, 0])
            xgT_copy(1, 1)
            hidden(0, 0)
            hidT_copy(0, 0)
            with dve.Fori(0, PAIRS) as i:
                with dve.If_lt(dve.to_reg(i), pairs):
                    for r in (1, 2):
                        t = 2 * i + r
                        dve.wait_ge(y_added, 32 * i + 16 * (r - 1))
                        dve.wait_ge(xgT_ready, t + 1)
                        V.tensor_copy(meta_y[:, r % 2], meta[:, r % 2])
                        xgT_copy(t + 1, (r + 1) % 2)
                        hidden(t, r % 2)
                        hidT_copy(t, r % 2)

        @block.tensor
        def _(pe):
            def mm(*a, **k):
                return nc.tensor.matmul(*a, **k)

            pe.wait_ge(const_in, 16)
            for hf in range(2):
                pe.wait_ge(xn_ready, 4 * hf + 4)
                for b in range(HB):
                    for n in range(4):
                        ins = nc.tensor.transpose(psum[:, 2 * hf + b, n * P:(n + 1) * P],
                                                  xn[:, 4 * hf + n, b * P:(b + 1) * P], ident)
                    ins.then_inc(xnT_ps, 1)
            for i, (w, hf) in enumerate(QK_IDX):
                pe.wait_ge(xnT_ready, 2 * hf + 2)
                pe.wait_ge(w_in[w], 16)
                if i >= 2:
                    pe.wait_ge(rope_mul, i - 1)
                for o in range(HB):
                    for b in range(HB):
                        ins = mm(psum[:, 4 + 2 * (i % 2) + o], wqkv[:, w, b, o * P:(o + 1) * P],
                                 xnT[:, b, cols(hf)], start=(b == 0), stop=(b == HB - 1))
                ins.then_inc(qk_ps, 1)
            pe.wait_ge(w_in[2], 16)
            pe.wait_ge(xnT_ready, 4)
            for n in range(TT):
                for b in range(HB):
                    ins = mm(psum[:, n // 2, (n % 2) * H:(n % 2 + 1) * H], xnT[:, b, n * P:(n + 1) * P],
                             wqkv[:, 2, b], start=(b == 0), stop=(b == HB - 1))
                if n % 2:
                    ins.then_inc(v_ps, 1)

            def lin_turn(b, g):
                pe.wait_ge(feat_ready, 1)
                pe.wait_ge(rope_mul, 4)
                for n in range(4):
                    ins = nc.tensor.transpose(psum[:, 4 + 2 * b + g, n * P:(n + 1) * P],
                                              kfeat[:, b, (4 * g + n) * P:(4 * g + n + 1) * P], ident)
                ins.then_inc(kft_ps, 1)

            def lin_state(b):
                pe.wait_ge(kft_ready, 2 * b + 2)
                pe.wait_ge(ones_set, 2)
                for n in range(TT):
                    ins = mm(psum[:, 4, b * LW:(b + 1) * LW], kfeat_tok[:, n, b * P:(b + 1) * P], v[:, n, b],
                             start=(n == 0), stop=(n == TT - 1))
                ins.then_inc(st_ps, 1)

            def lin_out(j):
                if j == 0:
                    pe.wait_ge(feat_ready, 2)
                    pe.wait_ge(st_ready, 1)
                if j == 3:
                    pe.wait_ge(mT_ready, 1)
                if j > 3:
                    pe.wait_ge(lin_ready, j - 1)
                for k, g in enumerate(LIN[j]):
                    n, b = g // HB, g % HB
                    ins = mm(psum[:, LIN_BANK[j], k * LW:(k + 1) * LW], qfeat[:, b, n * P:(n + 1) * P],
                             state[:, b], start=True, stop=True)
                ins.then_inc(lin_ps, 1)

            def score(i, t):
                u, s, _ = place(i, t)
                k, kh = s // 2, s % 2
                j, qb = k // 4, k % 4
                pair = STEPS * i + t // 2
                if s == 0:
                    pe.wait_ge(q_in, 16 * GROUPS * (u + 1))
                if kh == 0 and t >= 4:
                    pe.wait_ge(max_ready, pair - 1)
                ins = mm(psum[:, 2 * (k % 2) + kh], qst[0:SROWS, u % 4, j, qb * P:(qb + 1) * P],
                         kst[0:SROWS, u % NQ, j, cols(kh)], start=True, stop=True)
                if kh:
                    ins.then_inc(sc_ps, 1)

            def turn_max(u, first=False):
                pe.wait_ge(mhl_ready, 2 * u + 2)
                nc.tensor.transpose(psum[0:32, 7, 0:P // 2].bitcast(BF16),
                                    mhl.rearrange("p s k -> p (s k)"), ident_b).then_inc(mT_ps, 1)

            def score_t(i, t):
                u, r, n = place(i, t)
                kb, j = r // 4, r % 4
                if r == 0:
                    pe.wait_ge(mrow_in, 32 * (u + 1))
                if t >= 2:
                    pe.wait_ge(exp_ready, n - 1)
                mm(psum[:, 4 + t % 2], kst[0:SROWS + 2, u % NQ, j, kb * P:(kb + 1) * P],
                   qst[0:SROWS + 2, u % 4, j], start=True, stop=True).then_inc(sct_ps, 1)

            def product(i, g):
                u, kb = 2 * i + g // 8, g % 8
                pe.wait_ge(exp_ready, 2 * STEPS * i + 4 * g + 4)
                if kb == 0:
                    if g:
                        pe.wait_ge(osb_ready, u)
                    pe.wait_ge(v_staged, u + 1)
                for j in range(4):
                    ins = mm(psum[32 * j:32 * j + 32, 6], vst[:, g // 8 % 2, kb, j], prob[:, (4 * g + j) % 8],
                             start=(kb == 0), stop=(kb == 7), skip_group_check=True)
                ins.then_inc(av_ps, 1)

            def turn_o(u, par):
                pe.wait_ge(osb_ready, u + 1)
                pe.wait_ge(mT_ready, u + 2 if not isinstance(u, int) else min(u + 2, UNITS))
                if isinstance(u, int) and u == NQ:
                    pe.wait_ge(x2_ready, 2)
                if isinstance(u, int) and u == NQ + 1:
                    pe.wait_ge(slot_ready, 1)
                for b in range(4):
                    ins = nc.tensor.transpose(psum[:, 7, b * P:(b + 1) * P], osb[:, par, b * P:(b + 1) * P], ident)
                ins.then_inc(oT_ps, 1)

            def post(hf, f, k):
                if f == "combT":
                    pe.wait_ge(oT_read, 4 * (4 * hf + 4))
                    if k == 1 and not hf:
                        pe.wait_ge(combT_ready, 1)
                    for n in range(4):
                        ins = nc.tensor.transpose(psum[:, bank(hf, k), n * P:(n + 1) * P],
                                                  comb[:, n, k * P:(k + 1) * P], ident)
                    ins.then_inc(combT_ps, 1)
                if f == "wo":
                    pe.wait_ge(combT_ready, 2 * hf + 2)
                    pe.wait_ge(wo_in, 16)
                    if k and not hf:
                        pe.wait_ge(mT_ready, NQ + 2)
                    for n in range(2):
                        for b in range(HB):
                            ins = mm(psum[:, bank(hf, 2 + k), n * H:(n + 1) * H],
                                     combT[:, b, (2 * k + n) * P:(2 * k + n + 1) * P], wo[:, b],
                                     start=(b == 0), stop=(b == HB - 1))
                    ins.then_inc(wo_ps, 1)
                if f == "xn2T":
                    b = k - 2
                    pe.wait_ge(xn2_ready, 8 * (hf + 1))
                    if not hf:
                        pe.wait_ge(xn2T_ready, 1) if b else pe.wait_ge(oT_read, 4 * (NQ + 1))
                    for n in range(4):
                        ins = nc.tensor.transpose(psum[:, bank(hf, 4 + b), n * P:(n + 1) * P],
                                                  xn2[:, n, 0, b * P:(b + 1) * P], ident)
                    ins.then_inc(xn2T_ps, 1)
                if f == "logits":
                    pe.wait_ge(xn2T_ready, 2 * hf + 2)
                    pe.wait_ge(router_in, 16)
                    for n in range(4):
                        for b in range(HB):
                            ins = mm(psum[:, bank(hf, 6), n * E:(n + 1) * E], xn2T[:, b, n * P:(n + 1) * P],
                                     router[:, b], start=(b == 0), stop=(b == HB - 1))
                    ins.then_inc(lg_ps, 1)
                if f == "rank":
                    if not hf:
                        pe.wait_ge(mT_ready, NQ + 3)
                    pe.wait_ge(chosen_ready, hf + 1)
                    o = psum[:, bank(hf, 7), 0:4 * E]
                    c = chosen[:, 4 * hf:4 * hf + 4].rearrange("p n e -> p (n e)")
                    mm(o, tri_b, c, start=True, stop=False)
                    for n in range(4 * hf + 3):
                        m = max(n - 4 * hf + 1, 0)
                        ins = mm(o[:, m * E:].rearrange("p (n e) -> p n e", e=E), ones_b,
                                 chosen[:, n:n + 1].to_broadcast([P, 4 - m, E]), start=False,
                                 stop=(n == 4 * hf + 2))
                    if hf:
                        for n in range(TT):
                            ins = mm(psum[:, 5, 0:E], ones_b, chosen[:, n], start=(n == 0), stop=(n == TT - 1))
                    ins.then_inc(rank_ps, 1)

            pe.wait_ge(kst_set, 1)
            pe.wait_ge(identb_ready, 1)
            pe.wait_ge(v_ready, 4)
            pe.wait_ge(k0_in, 16 * GROUPS)
            for s in range(LEAD):
                score(0, s)
                if s in (20, 22, 24, 26):
                    lin_turn((s - 20) // 4, (s - 20) // 2 % 2)
                if s in (28, 32):
                    lin_state((s - 28) // 4)
                if s == 36:
                    pe.wait_ge(kft_ready, 4)
                    turn_max(0)
                if s in (38, 39, 40, 42):
                    lin_out((38, 39, 40, 42).index(s))
            pe.wait_ge(lin_ready, 2)
            pe.wait_ge(ones_set, 3)

            def steps(i, t):
                u, r, n = place(i, t)
                score_t(i, t)
                if not (isinstance(n, int) and n + LEAD >= ALL):
                    score(i, t + LEAD)
                if t in (1, 3):
                    lin_out(4 + t // 2)
                if t == 4:
                    pe.wait_ge(lin_ready, 5)
                if t % 4 == 1 and t > 1:
                    product(i, t // 4 - 1)
                if r == 8 and t > 8:
                    turn_o(u - 1, (t // STEPS - 1) % 2)
                if (t + LEAD) % STEPS == 3:
                    m = 2 * i + (t + LEAD) // STEPS - 1
                    if not (isinstance(n, int) and n + LEAD > ALL + 3):
                        pe.wait_ge(oT_read, 4 * (m - 1))
                        pe.wait_ge(lin_ready, 6)
                        if isinstance(m, int) and m == NQ + 1:
                            pe.wait_ge(x2_ready, 1)
                        if isinstance(m, int) and m == NQ + 2:
                            pe.wait_ge(lg_read, 1)
                        turn_max(m)
                if isinstance(n, int) and n in POST:
                    post(0, *POST[n])

            attention(pe, steps)
            product(NQ // 2, NQ * STEPS // 4 - 1)
            pe.wait_ge(oT_read, 4 * (UNITS - 1))
            turn_o(UNITS - 1, 1)
            for f, k in (("combT", 0), ("combT", 1), ("wo", 0), ("wo", 1), ("xn2T", 2), ("xn2T", 3),
                         ("logits", 0), ("rank", 0)):
                post(1, f, k)

            def load_expert(t):
                return pe.value_load(ex_i[0:1, bass.ts(t, 1)], min_val=0, max_val=E - 1)

            def gate_up(t, par, e, first=False):
                pe.wait_ge(xgT_ready, t + 1)
                if not first:
                    pe.wait_ge(hid_ready, t)
                for c in range(4):
                    for b in range(HB):
                        ins = mm(psum[:, c, 0:FN], xgT[:, par, b], gu[:, e, b, c * FN:(c + 1) * FN],
                                 start=(b == 0), stop=(b == HB - 1))
                ins.then_inc(gu_ps, 1)

            def turn_x(par, loads):
                pe.wait_ge(xg_in[par], 16 * loads)
                for b in range(HB):
                    ins = nc.tensor.transpose(psum[:, 7, b * P:(b + 1) * P], xg[:, par, b * P:(b + 1) * P], ident)
                ins.then_inc(xgT_ps, 1)

            def turn_hidden(t, par):
                pe.wait_ge(hid_ready, t + 1)
                for c, (o, n) in enumerate(zip(FO, FB)):
                    ins = nc.tensor.transpose(psum[0:n, 4 + c // 4, (c % 4) * P:(c % 4 + 1) * P],
                                              hid[:, par, o:o + n], ident)
                ins.then_inc(hidT_ps, 1)

            def down(t, par, e):
                pe.wait_ge(hidT_ready, t + 1)
                pe.wait_ge(y_ready, t)
                for c, n in enumerate(FB):
                    ins = mm(psum[:, 6, 0:H], hidT[0:n, par, c], dn[0:n, c, e], start=(c == 0),
                             stop=(c == len(FB) - 1))
                ins.then_inc(y_ps, 1)

            pe.wait_ge(expert_ready, 2)
            pairs = pe.value_load(pairs_i[0:1, 0:1], min_val=1, max_val=PAIRS)
            turn_x(0, 1)
            pe.wait_ge(xgT_ready, 1)
            turn_x(1, 1)
            pe.wait_ge(gu_in, 16 * E)
            gate_up(0, 0, load_expert(0), first=True)
            turn_hidden(0, 0)
            pe.wait_ge(dn_in, 16 * len(FB))
            with pe.Fori(0, PAIRS) as i:
                with pe.If_lt(pe.to_reg(i), pairs):
                    for r in (1, 2):
                        t = 2 * i + r
                        gate_up(t, r % 2, load_expert(t))
                        turn_x((r + 1) % 2, i + 2)
                        down(t - 1, (r + 1) % 2, load_expert(t - 1))
                        turn_hidden(t, r % 2)
            down(2 * pairs, 0, load_expert(2 * pairs))


def kernel(**inputs):
    from concourse import bacc
    from concourse.bass_utils import run_bass_kernel_spmd

    f = {n.removeprefix("L0_"): np.asarray(a) for n, a in inputs.items()}
    rows = lambda w: w.T.reshape(HB, P, -1).transpose(1, 0, 2)
    weights = np.stack([rows(f[n]) for n in ("attn_Wk", "attn_Wq", "attn_Wv", "attn_Wo")], 1)
    gate_up = np.concatenate([f["ffn_gate_w"], f["ffn_up_w"]], 1)
    const, rope = constants()
    arrays = {
        "x": f["attn_hidden_states"],
        "weights": weights,
        "rope": rope,
        "const": const,
        "gate": f["attn_gate"].reshape(1, NH),
        "router": rows(f["ffn_router_w"]),
        "gate_up": gate_up.transpose(2, 0, 1).reshape(HB, P, E, 2 * F).transpose(1, 2, 0, 3),
        "down": f["ffn_down_w"].transpose(2, 0, 1),
    }
    arrays = {n: np.ascontiguousarray(a) for n, a in arrays.items()}
    nc = bacc.Bacc("TRN2", target_bir_lowering=False, num_devices=1)
    args = [nc.dram_tensor(n, a.shape, mybir.dt.from_np(a.dtype), kind="ExternalInput").ap()
            for n, a in arrays.items()]
    args.append(nc.dram_tensor("out", [1, T, H], F32, kind="ExternalOutput").ap())
    block_kernel(nc, *args)
    return run_bass_kernel_spmd(nc, [arrays], core_ids=[0]).results[0]["out"]
```

```python
from contextlib import ExitStack

import concourse.bass as bass
from concourse import mybir
from concourse.alu_op_type import AluOpType as ALU
import numpy as np

ACT = mybir.ActivationFunctionType
F32, BF16, U32, I32 = mybir.dt.float32, mybir.dt.bfloat16, mybir.dt.uint32, mybir.dt.int32
AX = mybir.AxisListType

P = 128
T, H, NH = 1024, 256, 16
HD = H // NH
TT, HB = T // P, H // P
HALF = T // 2
E, F, K = 8, 688, 2
FB = [P, P, P, P, 88, 88]
FO = [sum(FB[:i]) for i in range(len(FB))]
FN = F // 2
NTILE = (K * T + E * (P - 1)) // P
EARLY = 2
PAIRS = (EARLY + NTILE - 1) // 2
NSLOT = (E * T) + P
ROW = H + 2
EPS = 1e-5
NQ = NH // 4
UNITS = 2 * NQ
STEPS = 32
GROUPS = 6
QPART = [0, 0, 1, 1, 0, 2]
KPART = [0, 1, 0, 1, 2, 0]
SROWS = GROUPS * HD
LEAD = 44
PEEL = 11

C_ID, C_MASK, C_TRI, C_LTI, C_J, C_IOTA = 0, 128, 256, 384, 448, 512
C_EVEN = C_IOTA + E
C_ROW0 = C_EVEN + PAIRS
C_PAD = C_ROW0 + NTILE + 1
C_TOK = C_PAD + 1
C_LIST = C_TOK + TT
C_TAU = C_LIST + E
NCONST = C_TAU + (NTILE + 1) * E


def constants():
    c = np.zeros((P, NCONST), np.float32)
    p = np.arange(P)
    c[:, C_ID:C_ID + P] = np.eye(P)
    c[:, C_MASK:C_MASK + P] = p[:, None] // HD == p[None] // HD
    c[:, C_TRI:C_TRI + P] = p[:, None] < p[None]
    e = np.arange(E)
    c[:, C_LTI:C_LTI + E * E] = (e[None] <= e[:, None]).reshape(-1)
    c[:, C_J:C_J + E * E] = np.tile(np.arange(T // P) * P, E)
    c[:, C_IOTA:C_IOTA + E] = e
    c[:, C_EVEN:C_EVEN + PAIRS] = 2 * np.arange(1, PAIRS + 1) + 1 - EARLY
    c[:, C_ROW0:C_ROW0 + NTILE + 1] = np.arange(NTILE + 1)
    c[:, C_PAD] = T + p
    c[:, C_TOK:C_TOK + TT] = np.arange(TT) * P + p[:, None]
    c[:, C_LIST:C_LIST + E] = e * T
    c[:, C_TAU:] = np.repeat(np.arange(NTILE + 1), E)
    inv_freq = np.float32(1) / np.float32(10000) ** (np.arange(0, H, 2, dtype=np.float32) / np.float32(H))
    angle = inv_freq[:, None] * np.arange(T, dtype=np.float32)[None]
    return c, np.stack([np.cos(angle), np.sin(angle)], 1).astype(np.float32)


def block_kernel(nc, x_d, w_d, rope_d, const_d, gate_d, router_d, gu_d, dn_d, out_d):
    ctx = ExitStack()
    with ctx:
        WORDS = 53200
        mem = ctx.enter_context(nc.sbuf_tensor("mem", [P, WORDS], F32))
        psum = ctx.enter_context(nc.psum_tensor("psum", [P, 8, 512], F32))

        def words(at, *shape, dt=F32, parts=P):
            n = int(np.prod(shape))
            v = mem[0:parts, at:at + (n if dt != BF16 else n // 2)]
            if dt != F32:
                v = v.bitcast(dt)
            names = "abcd"[:len(shape)]
            if len(shape) > 1:
                v = v.rearrange(f"p ({' '.join(names)}) -> p {' '.join(names)}",
                                **dict(zip(names, shape)))
            return v

        G = 0
        gu = words(G, E, HB, 2 * F)
        xn = words(G, TT, H)
        kfeat_tok = words(G, TT, H)
        xnT = words(G + 2048, HB, T)
        qfeat = words(G + 2048, HB, T)
        rope = words(G + 4096, 2, T)
        relu = words(G + 4096, HB, T)
        wqkv = words(G + 6144, 3, HB, H)
        kT = words(G + 7680, HB, T)
        qT = words(G + 9728, HB, T)
        parts = words(G + 11776, 2, 3, HB, T, dt=BF16)
        tmp = words(G + 17920, 4, HALF)
        kfeat = words(G + 19968, HB, T)
        late = G + (E - 1) * HB * 2 * F
        osb = words(late, 2, HALF)
        combT = words(late + 1024, HB, HALF)
        xn2T = words(late + 1024, HB, HALF)
        A = E * HB * 2 * F
        dn = words(A, len(FB), E, H)
        kst = words(A, NQ, 4, T, dt=BF16)
        qst = words(A + 8192, 4, 4, HALF, dt=BF16)
        prob = words(A + 12288, 8, HALF)
        resid = words(A + 12288, 2, HB, HALF)
        tmp_odd = words(A + 14336, 4, HALF)
        at = [A + 16384]

        def keep(*shape, dt=F32, parts=P):
            n = int(np.prod(shape))
            n = n if dt != BF16 else (n + 1) // 2
            v = words(at[0], *shape, dt=dt, parts=parts)
            at[0] += n
            return v

        x = keep(TT, H)
        b_v = at[0]
        v = keep(TT, HB, P + 8)
        vst = keep(2, TT, 4, 32)
        lin = keep(TT, H)
        b_end = at[0]
        comb = keep(4, H)
        wo = keep(HB, H)
        const = keep(NCONST)
        xn2 = keep(4, K, ROW)
        ident_b = keep(P, dt=BF16)
        state = keep(HB, P + 8)
        stat = keep(TT, 6)
        mv = keep(TT, 2)
        rstd = keep(TT)
        gate = keep(NH)
        gate_e = keep(NH)
        gate_1 = keep(NH)
        omg = keep(NH)
        half_c = keep(TT)
        gate_2 = keep(2, NH)
        lin_r = keep(3, 8)
        lin_g = keep(3, 8)
        den_r = keep(4, 4)
        den_g = keep(4, 4)
        mx = keep(2, 16)
        mhl = keep(2, 16, dt=BF16)
        mT = keep(P, dt=BF16, parts=32)
        router = keep(HB, E)
        lg = keep(4, E)
        top = keep(4, 8)
        topi = keep(4, 8, dt=U32)
        topf = keep(4, K)
        onehot = keep(K, 4, E)
        chosen = keep(TT, E, dt=BF16)
        tri_b = keep(P, dt=BF16)
        ones_b = keep(P, dt=BF16)
        pw_d = keep(4)
        pw_e = keep(4)
        pw_s = keep(4)
        cnt = keep(E)
        cmp = keep(E, E)
        tiles = keep(E)
        cum = keep(E)
        pos = keep(4, E)
        sel = keep(K, 4, E)
        slot_f = keep(K, 4)
        slot = keep(2, K, 4, dt=U32)
        tau = keep(NTILE + 1, E)
        tau_n = keep(NTILE + 1, E)
        ex_f = keep(NTILE + 1)
        ex_n = keep(NTILE + 1)
        ex_r = keep(NTILE + 1)
        ex_i = keep(EARLY + NTILE + 1, dt=I32)
        row_i = keep(EARLY + NTILE + 1, dt=I32)
        full = keep(E)
        cum_0 = keep(E)
        take = keep(E + 1)
        left_tiles = keep(E)
        delta = keep(E)
        tau_0 = keep(EARLY, E)
        ex_0 = keep(EARLY)
        even = keep(PAIRS)
        pairs_f = keep(1)
        left_f = keep(1)
        pairs_i = keep(2, dt=I32)
        meta = keep(2, 2, dt=U32)
        meta_y = keep(2, 2, dt=U32)
        assert at[0] <= WORDS, at[0]
        at[0] = b_v
        xg = keep(2, ROW)
        xgT = keep(2, HB, P)
        act_g = keep(2, F)
        hid = keep(2, F)
        hidT = keep(2, len(FB), P)
        yt = keep(2, H)
        assert at[0] <= b_end, at[0] - b_end
        ident = const[:, C_ID:C_ID + P]

        parts_d = nc.dram_tensor("parts_d", [2, 3, H, T], BF16).ap()
        xg_d = nc.dram_tensor("xg_d", [NSLOT, ROW], F32).ap()
        sum_d = nc.dram_tensor("sum_d", [T + P, H], F32).ap()

        def sem(name):
            return ctx.enter_context(nc.semaphore(name))

        x_in = [sem(f"x_in{i}") for i in range(4)]
        w_in = [sem(f"w_in{i}") for i in range(3)]
        rope_in, ident_in, const_in, gate_in, wo_in, router_in = (sem(n) for n in
            ("rope_in", "ident_in", "const_in", "gate_in", "wo_in", "router_in"))
        ones_set, kst_set, xg_set, xg_filled = (sem(n) for n in ("ones_set", "kst_set", "xg_set", "xg_filled"))
        identb_ready = sem("identb_ready")
        dve_step = sem("dve_step")
        var_ready, rstd_ready, xn_ready, xnT_ps, xnT_ready = (sem(n) for n in
            ("var_ready", "rstd_ready", "xn_ready", "xnT_ps", "xnT_ready"))
        qk_ps, rope_mul, rope_ready = sem("qk_ps"), sem("rope_mul"), sem("rope_ready")
        hi_ready, res_ready, mid_ready, lo_ready = (sem(n) for n in ("hi_ready", "res_ready", "mid_ready", "lo_ready"))
        part_out = [[sem(f"part_out{i}_{s}") for s in range(3)] for i in range(4)]
        v_ps, v_ready = sem("v_ps"), sem("v_ready")
        neg_ready, relu_ready, nexp_ready, feat_ready = (sem(n) for n in
            ("neg_ready", "relu_ready", "nexp_ready", "feat_ready"))
        kft_ps, kft_ready, st_ps, st_ready, lin_ps, lin_ready = (sem(n) for n in
            ("kft_ps", "kft_ready", "st_ps", "st_ready", "lin_ps", "lin_ready"))
        gexp_ready = sem("gexp_ready")
        k0_in, k_in, q_in = sem("k0_in"), sem("k_in"), sem("q_in")
        sc_ps, max_ready, mhl_ready, mT_ps, mT_ready, mrow_in = (sem(n) for n in
            ("sc_ps", "max_ready", "mhl_ready", "mT_ps", "mT_ready", "mrow_in"))
        sct_ps, exp_ready, av_ps, osb_ready, v_staged = (sem(n) for n in
            ("sct_ps", "exp_ready", "av_ps", "osb_ready", "v_staged"))
        oT_ps, oT_read = sem("oT_ps"), sem("oT_read")
        combT_ps, combT_ready, wo_ps, x2_ready, xn2_ready, xn2T_ps, xn2T_ready = (sem(n) for n in
            ("combT_ps", "combT_ready", "wo_ps", "x2_ready", "xn2_ready", "xn2T_ps", "xn2T_ready"))
        lg_ps, lg_read, top_ready, pexp_ready, chosen_ready, rank_ps = (sem(n) for n in
            ("lg_ps", "lg_read", "top_ready", "pexp_ready", "chosen_ready", "rank_ps"))
        slot_ready, early_ready, expert_ready = (sem(n) for n in ("slot_ready", "early_ready", "expert_ready"))
        sum_init, scattered = sem("sum_init"), [sem("scattered0"), sem("scattered1")]
        gu_in, dn_in = sem("gu_in"), sem("dn_in")
        xg_in = [sem("xg_in0"), sem("xg_in1")]
        xgT_ps, xgT_ready, gu_ps, silu_ready, hid_ready = (sem(n) for n in
            ("xgT_ps", "xgT_ready", "gu_ps", "silu_ready", "hid_ready"))
        hidT_ps, hidT_ready, y_ps, y_ready, y_taken, y_added = (sem(n) for n in
            ("hidT_ps", "hidT_ready", "y_ps", "y_ready", "y_taken", "y_added"))
        out_done = sem("out_done")

        QK_IDX = [(0, 0), (0, 1), (1, 0), (1, 1)]
        x_v = x_d.rearrange("o (n p) h -> p (o n) h", p=P)
        pv = parts_d.rearrange("w s (b p) t -> w s p b t", p=P)
        banks = lambda i, n: psum[:, i:i + n, :].rearrange("p b c -> p (b c)")
        cols = lambda hf: slice(hf * HALF, (hf + 1) * HALF)
        ALL = STEPS * UNITS

        def attention(eng, steps):
            for t in range(PEEL):
                steps(0, t)
            with eng.Fori(0, NQ // 2) as i:
                for t in range(PEEL, 2 * STEPS + PEEL):
                    steps(i, t)
            for t in range(PEEL, NQ * STEPS):
                steps(NQ // 2, t)

        LW = P + 8
        LIN = [list(range(g, min(g + 3, HB * TT))) for g in range(0, HB * TT, 3)]
        LIN_BANK = [4, 5, 6, 7, 6, 7]
        LIN_STEP = [29, 31, 33, 39, 41, 43]

        def bank(hf, idx):
            return (4, 0, 5, 4, 6, 4, 5, 6)[idx] if hf else 7

        LAST = STEPS * (UNITS - 1)

        def score_bank(n, t):
            return n % 4 if isinstance(n, int) and n >= LAST else 4 + t % 2

        POST = {NQ * STEPS + n: w for n, w in {
            13: (0, "combT", 0), 14: (0, "copy", 0), 15: (0, "combT", 1), 16: (0, "copy", 1),
            18: (0, "wo", 0), 19: (0, "add", 0), 27: (0, "wo", 1), 28: (0, "add", 1), 31: (0, "norm", 0),
            STEPS + 12: (0, "xn2T", 2), STEPS + 13: (0, "copy", 2), STEPS + 14: (0, "xn2T", 3),
            STEPS + 15: (0, "copy", 3), STEPS + 17: (0, "logits", 0), STEPS + 18: (0, "choose", 0),
            STEPS + 20: (0, "top", 0), STEPS + 28: (0, "rank", 0), STEPS + 29: (0, "place", 0),
            3 * STEPS + 13: (1, "combT", 0), 3 * STEPS + 15: (1, "copy", 0),
            3 * STEPS + 19: (1, "wo", 0), 3 * STEPS + 23: (1, "wo", 1)}.items()}

        def place(i, t):
            return 2 * i + t // STEPS, t % STEPS, 2 * STEPS * i + t

        block = ctx.enter_context(nc.Block())

        @block.sync
        def _(sp):
            for i in range(4):
                sp.dma_start(x[:, 2 * i:2 * i + 2, :], x_v[:, 2 * i:2 * i + 2, :]).then_inc(x_in[i], 16)
                if i == 0:
                    sp.dma_start(ident, const_d[:, 0:P]).then_inc(ident_in, 16)
            sp.dma_start(const[:, P:], const_d[:, P:]).then_inc(const_in, 16)
            sp.dma_start(wqkv[:, 1], w_d[:, 1]).then_inc(w_in[1], 16)
            sp.dma_start(wo, w_d[:, 3]).then_inc(wo_in, 16)
            sp.dma_start(router, router_d).then_inc(router_in, 16)

            def parts_out(i):
                w, hf = QK_IDX[i]
                for s, ready in enumerate((hi_ready, mid_ready, lo_ready)):
                    sp.wait_ge(ready, i + 1)
                    sp.dma_start(pv[w, s][:, :, cols(hf)], parts[:, w, s, :, cols(hf)]).then_inc(part_out[i][s], 16)

            def k_stack(qd, done):
                for g in range(GROUPS):
                    src = parts_d[0, KPART[g]].rearrange("(q j r) t -> q r j t", j=4, r=HD)[qd]
                    sp.dma_start(kst[g * HD:(g + 1) * HD, qd], src).then_inc(done, 16)

            def q_stack(qd, hf, sl, groups=range(GROUPS)):
                for g in groups:
                    src = parts_d[1, QPART[g]].rearrange("(q j r) t -> q r j t", j=4, r=HD)[qd]
                    sp.dma_start(qst[g * HD:(g + 1) * HD, sl], src[:, :, cols(hf)]).then_inc(q_in, 16)

            def max_rows(u, sl):
                sp.wait_ge(mT_ready, u + 1)
                for s in range(2):
                    dst = qst[SROWS + s:SROWS + s + 1, sl].rearrange("p j q -> p (j q)")
                    sp.dma_start(dst, mT[16 * s:16 * s + 16]).then_inc(mrow_in, 16)

            parts_out(0)
            parts_out(1)
            for i in range(2):
                for s in range(3):
                    sp.wait_ge(part_out[i][s], 16)
            k_stack(0, k0_in)
            parts_out(2)
            for s in range(3):
                sp.wait_ge(part_out[2][s], 16)
                q_stack(0, 0, 0, [g for g in range(GROUPS) if QPART[g] == s])
            for qd in range(1, NQ):
                k_stack(qd, k_in)
                sp.wait_ge(k_in, 16 * GROUPS * qd)
                sp.wait_ge(q_in, 16 * GROUPS * qd)
                q_stack(qd, 0, qd)
            parts_out(3)
            for s in range(3):
                sp.wait_ge(part_out[3][s], 16)
            max_rows(0, 0)
            max_rows(1, 1)
            with sp.Fori(1, NQ + 1) as u:
                sp.wait_ge(exp_ready, STEPS * u)
                sp.wait_ge(q_in, 16 * GROUPS * (u + 3))
                q_stack(u - 1, 1, (u + 3) % 4)
                max_rows(u + 1, (u + 1) % 4)
            for u in (UNITS - 2, UNITS - 1):
                max_rows(u, u % 4)

            def start_sum(hf):
                sp.wait_ge(x2_ready, 2 * hf + 2)
                sp.dma_start(sum_d[hf * HALF:(hf + 1) * HALF].rearrange("(n p) h -> p n h", p=P),
                             x[:, 4 * hf:4 * hf + 4]).then_inc(sum_init, 16)

            def load_xg(t, par):
                row = sp.value_load(row_i[0:1, bass.ts(t, 1)], min_val=0, max_val=E * T)
                sp.dma_start(xg[:, par], xg_d[bass.ds(row, P), :]).then_inc(xg_in[par], 16)

            start_sum(0)
            sp.dma_start(sum_d[T:], x[:, 0]).then_inc(sum_init, 16)
            sp.wait_ge(v_staged, UNITS)
            sp.wait_ge(early_ready, 2)
            sp.wait_ge(scattered[0], 16 * K * 4)
            for t in range(EARLY):
                load_xg(t, t)
            start_sum(1)
            sp.wait_ge(scattered[1], 16 * K * 4)
            sp.wait_ge(expert_ready, 2)
            pairs = sp.value_load(pairs_i[0:1, 0:1], min_val=1, max_val=PAIRS)
            left = sp.value_load(pairs_i[0:1, 1:2], min_val=0, max_val=1)
            with sp.Fori(0, PAIRS) as i:
                with sp.If_lt(sp.to_reg(i), pairs):
                    for r in (1, 2):
                        t = 2 * i + r
                        sp.wait_ge(xgT_ready, t)
                        load_xg(t + 1, (r + 1) % 2)
            sp.wait_ge(y_added, 32 * pairs + 16 * left + 16)
            sp.dma_start(out_d.rearrange("o (p n) h -> p (o n h)", p=P),
                         sum_d[0:T].rearrange("(p n) h -> p (n h)", p=P)).then_inc(out_done, 16)
            sp.wait_ge(out_done, 16)

        @block.gpsimd
        def _(pool):
            pool.memset(half_c, -0.5).then_inc(ones_set, 1)
            pool.memset(v[:, :, :, P:].rearrange("p n b c -> p (n b) c"), 1.0).then_inc(ones_set, 1)
            pool.memset(vst.rearrange("p a n j c -> p (a n j c)"), 1.0).then_inc(ones_set, 1)
            pool.wait_ge(ones_set, 3)

            def reciprocal_root(c, n):
                pool.wait_ge(var_ready, n)
                nc.gpsimd.tensor_tensor(rstd[:, c], rstd[:, c], half_c[:, c], ALU.pow).then_inc(rstd_ready, 1)

            for g in range(4):
                reciprocal_root(slice(2 * g, 2 * g + 2), g + 1)
            two = float(np.array(0xBF80BF80, np.uint32).view(np.float32))
            pool.wait_ge(rstd_ready, 4)
            pool.memset(mem[SROWS:SROWS + 2, A:A + 2 * NQ * T], two).then_inc(kst_set, 1)
            pool.wait_ge(kst_set, 1)
            for i, (w, hf) in enumerate(QK_IDX):
                o, c = (kT, qT)[w], cols(hf)
                pool.wait_ge(rope_mul, i + 1)
                m = (tmp, tmp_odd)[i % 2]
                nc.gpsimd.tensor_tensor(o[:, 0, c], m[:, 0], m[:, 1], ALU.subtract)
                nc.gpsimd.tensor_tensor(o[:, 1, c], m[:, 2], m[:, 3], ALU.add).then_inc(rope_ready, 1)
            tv = tmp.rearrange("p (b h) c -> p b (h c)", b=HB)
            for i, dst in enumerate((kfeat, qfeat)):
                pool.wait_ge(relu_ready, i + 1)
                pool.wait_ge(nexp_ready, i + 1)
                if i == 1:
                    pool.wait_ge(v_ps, 4)
                nc.gpsimd.tensor_tensor(dst, relu, tv, ALU.add).then_inc(feat_ready, 1)

            def stage_v(u, sl, qd):
                c = qd % 2 * 4 * HD
                src = v[:, :, qd // 2, c:c + 4 * HD].rearrange("p n (j c) -> p n j c", c=HD)
                nc.gpsimd.tensor_copy(vst[:, sl, :, :, 0:HD], src).then_inc(v_staged, 1)

            pool.wait_ge(v_ready, 4)
            stage_v(0, 0, 0)
            stage_v(1, 1, 1)
            pool.wait_ge(xg_set, 1)
            pool.wait_ge(lin_ps, len(LIN))
            for i in range(4):
                for s in range(3):
                    pool.wait_ge(part_out[i][s], 16)

            def fill(lo, hi):
                pool.dma_start(xg_d[lo:hi].rearrange("(n p) h -> p n h", p=P),
                               xn2[:, 0, 0:1].to_broadcast([P, (hi - lo) // P, ROW])).then_inc(xg_filled, 16)

            for e in range(E):
                for m in range(2):
                    pool.wait_ge(av_ps, 4 * (e - e % 2) + 2 * (e % 2) + m + 1)
                    if m == 0:
                        fill(e * T, (e + 1) * T)
                    elif e < E - 1:
                        pool.dma_start(gu[:, e], gu_d[:, e]).then_inc(gu_in, 16)
                    else:
                        fill(E * T, NSLOT)
                if e in (2, 4, 6):
                    u = e // 2 + 1
                    stage_v(u, u % 2, u % NQ)
            pool.wait_ge(av_ps, 8 * NQ)
            stage_v(NQ + 1, (NQ + 1) % 2, 1)

            def scatter(hf):
                pool.wait_ge(slot_ready, hf + 1)
                for n in range(4):
                    for k in range(K):
                        pool.indirect_dma_start(
                            out=xg_d, out_offset=bass.IndirectOffsetOnAxis(ap=slot[:, hf, k, n:n + 1], axis=0),
                            in_=xn2[:, n, k], in_offset=None).then_inc(scattered[hf], 16)

            reciprocal_root(slice(0, 4), 5)
            for u in (UNITS - 2, UNITS - 1):
                pool.wait_ge(av_ps, 8 * (u - 1))
                stage_v(u, u % 2, u % NQ)
            pool.wait_ge(xg_filled, 16 * (E + 1))
            scatter(0)
            pool.wait_ge(sct_ps, ALL)
            for c, (o, n) in enumerate(zip(FO, FB)):
                pool.dma_start(dn[0:n, c], dn_d[o:o + n]).then_inc(dn_in, 16)
            reciprocal_root(slice(4, 8), 6)
            pool.wait_ge(lg_ps, 2)
            pool.dma_start(gu[:, E - 1], gu_d[:, E - 1]).then_inc(gu_in, 16)
            scatter(1)

            pool.wait_ge(sum_init, 48)
            def add_y(t, par):
                pool.wait_ge(y_added, 16 * t)
                pool.wait_ge(y_ready, t + 1)
                pool.sem_inc(y_taken, 1)
                pool.indirect_dma_start(
                    out=sum_d, out_offset=bass.IndirectOffsetOnAxis(ap=meta_y[:, par, 1:2], axis=0),
                    in_=yt[:, par], in_offset=None, compute_op=ALU.add).then_inc(y_added, 16)

            pool.wait_ge(expert_ready, 2)
            pairs = pool.value_load(pairs_i[0:1, 0:1], min_val=1, max_val=PAIRS)
            left = pool.value_load(pairs_i[0:1, 1:2], min_val=0, max_val=1)
            with pool.Fori(0, PAIRS) as i:
                with pool.If_lt(pool.to_reg(i), pairs):
                    for r in (0, 1):
                        add_y(2 * i + r, r)
            add_y(2 * pairs, 0)
            with pool.If(left):
                add_y(2 * pairs + 1, 1)

        @block.scalar
        def _(act):
            act.dma_start(wqkv[:, 0], w_d[:, 0]).then_inc(w_in[0], 16)
            act.dma_start(gate, gate_d.to_broadcast([P, NH])).then_inc(gate_in, 16)
            act.wait_ge(x_in[3], 16)
            act.dma_start(rope, rope_d).then_inc(rope_in, 16)
            act.dma_start(wqkv[:, 2], w_d[:, 2]).then_inc(w_in[2], 16)
            act.wait_ge(gate_in, 16)
            nc.scalar.activation(gate_e, gate, ACT.Exp, scale=-1.0).then_inc(gexp_ready, 1)
            for hf in range(2):
                for b in range(HB):
                    act.wait_ge(xnT_ps, 2 * hf + b + 1)
                    nc.scalar.copy(xnT[:, b, cols(hf)], psum[:, 2 * hf + b]).then_inc(xnT_ready, 1)
            for i, (w, hf) in enumerate(QK_IDX):
                act.wait_ge(rope_ready, i + 1)
                nc.scalar.copy(parts[:, w, 0, :, cols(hf)], (kT, qT)[w][:, :, cols(hf)]).then_inc(hi_ready, 1)
                if i == 2:
                    act.wait_ge(v_ps, 2)
                    for j in range(2):
                        nc.scalar.copy(v[:, 2 * j:2 * j + 2, :, 0:P],
                                       psum[:, j].rearrange("p (n b c) -> p n b c", n=2, b=HB)).then_inc(v_ready, 1)
                act.wait_ge(res_ready, i + 1)
                nc.scalar.copy(parts[:, w, 1, :, cols(hf)], resid[:, i % 2]).then_inc(mid_ready, 1)
                if i == 2:
                    act.wait_ge(v_ps, 4)
                    for j in range(2, 4):
                        nc.scalar.copy(v[:, 2 * j:2 * j + 2, :, 0:P],
                                       psum[:, j].rearrange("p (n b c) -> p n b c", n=2, b=HB)).then_inc(v_ready, 1)
            for i in range(2):
                act.wait_ge(rope_mul, 4) if i == 0 else act.wait_ge(feat_ready, 1)
                nc.scalar.activation(relu, (kT, qT)[i], ACT.Relu).then_inc(relu_ready, 1)
                act.wait_ge(neg_ready, i + 1)
                nc.scalar.activation(tmp, tmp, ACT.Exp).then_inc(nexp_ready, 1)
            for i in range(4):
                b, g = i // 2, i % 2
                act.wait_ge(kft_ps, i + 1)
                nc.scalar.copy(kfeat_tok[:, 4 * g:4 * g + 4, b * P:(b + 1) * P],
                               psum[:, 4 + i].rearrange("p (n c) -> p n c", n=4)).then_inc(kft_ready, 1)

            def turned_copy(hf, n):
                if n < 2:
                    act.wait_ge(combT_ps, 2 * hf + n + 1)
                    nc.scalar.copy(combT[:, n], psum[:, bank(hf, n)]).then_inc(combT_ready, 1)
                else:
                    act.wait_ge(xn2T_ps, 2 * hf + n - 1)
                    nc.scalar.copy(xn2T[:, n - 2], psum[:, bank(hf, n + 2)]).then_inc(xn2T_ready, 1)

            def second_exp(hf):
                act.wait_ge(top_ready, hf + 1)
                nc.scalar.activation(pw_e, pw_d, ACT.Exp).then_inc(pexp_ready, 1)

            def osb_copy(u, par):
                act.wait_ge(av_ps, 8 * u + 8)
                nc.scalar.copy(osb[:, par], psum[:, 6]).then_inc(osb_ready, 1)

            def steps(i, t):
                u, r, n = place(i, t)
                if t % 4 == 0 and t >= 8:
                    act.wait_ge(av_ps, 16 * i + t // 4 - 1)
                act.wait_ge(sct_ps, n + 1)
                nc.scalar.activation(prob[:, t % 8], psum[:, score_bank(n, t)], ACT.Exp,
                                     scale=HD ** -0.5).then_inc(exp_ready, 1)
                if r == 3 and t > 3:
                    osb_copy(u - 1, (t // STEPS - 1) % 2)
                if isinstance(n, int) and n in POST:
                    hf, f, k = POST[n]
                    if f == "copy":
                        turned_copy(hf, k)
                    if f == "top":
                        second_exp(0)

            attention(act, steps)
            osb_copy(UNITS - 1, 1)
            turned_copy(1, 1)
            turned_copy(1, 2)
            turned_copy(1, 3)
            second_exp(1)

            def silu(t, par):
                act.wait_ge(gu_ps, t + 1)
                nc.scalar.activation(act_g[:, par].rearrange("p (b c) -> p b c", b=2),
                                     psum[:, 0:2, 0:FN], ACT.Silu).then_inc(silu_ready, 1)

            def weigh(t, par):
                act.wait_ge(y_ps, t + 1)
                nc.scalar.activation(yt[:, par], psum[:, 6, 0:H], ACT.Copy,
                                     scale=meta_y[:, par, 0:1].bitcast(F32)).then_inc(y_ready, 1)

            silu(0, 0)
            act.wait_ge(expert_ready, 2)
            pairs = act.value_load(pairs_i[0:1, 0:1], min_val=1, max_val=PAIRS)
            left = act.value_load(pairs_i[0:1, 1:2], min_val=0, max_val=1)
            with act.Fori(0, PAIRS) as i:
                with act.If_lt(act.to_reg(i), pairs):
                    for r in (1, 2):
                        t = 2 * i + r
                        silu(t, r % 2)
                        act.wait_ge(y_added, 32 * i)
                        weigh(t - 1, (r + 1) % 2)
            with act.If(left):
                silu(2 * pairs + 1, 1)
            act.wait_ge(y_added, 32 * pairs)
            weigh(2 * pairs, 0)
            with act.If(left):
                weigh(2 * pairs + 1, 1)

        @block.vector
        def _(dve):
            V = nc.vector
            chain = [0]

            def link(ins):
                chain[0] += 1
                ins.then_inc(dve_step, 1)
                dve.wait_ge(dve_step, chain[0])

            def spreads(lo, hi):
                for n in range(lo, hi):
                    ins = V.bn_aggr(mv[:, n], stat[:, n])
                link(ins)
                V.tensor_scalar(rstd[:, lo:hi], mv[:, lo:hi, 1], EPS, None, ALU.add).then_inc(var_ready, 1)

            def normalise(i):
                dve.wait_ge(rstd_ready, i + 1)
                for n in (2 * i, 2 * i + 1):
                    V.tensor_scalar(xn[:, n], x[:, n], mv[:, n, 0:1], rstd[:, n:n + 1],
                                    ALU.subtract, ALU.mult).then_inc(xn_ready, 1)

            for i in range(4):
                dve.wait_ge(x_in[i], 16)
                for n in (2 * i, 2 * i + 1):
                    ins = V.bn_stats(stat[:, n], x[:, n])
                link(ins)
                spreads(2 * i, 2 * i + 2)
                if i:
                    normalise(i - 1)
            normalise(3)
            dve.wait_ge(ident_in, 16)
            dve.wait_ge(const_in, 16)
            V.tensor_copy(ident_b, ident).then_inc(identb_ready, 1)
            V.tensor_copy(tri_b, const[:, C_TRI:C_TRI + P])
            V.memset(ones_b, 1.0)
            V.memset(xn2[:, 0, 0, 0:H + 1], 0.0)
            V.tensor_copy(xn2[:, 0, 0, H + 1:ROW].bitcast(U32), const[:, C_PAD:C_PAD + 1]).then_inc(xg_set, 1)
            dve.wait_ge(gexp_ready, 1)
            link(V.tensor_scalar(gate_1, gate_e, 1.0, None, ALU.add))
            link(V.reciprocal(gate, gate_1))
            for k in range(2):
                V.tensor_copy(gate_2[:, k], gate)
            link(V.tensor_tensor(omg, gate, gate_e, ALU.mult))
            dve.wait_ge(rope_in, 16)

            def split(i):
                w, hf = QK_IDX[i]
                dve.wait_ge(hi_ready, i + 1)
                V.tensor_tensor(resid[:, i % 2], (kT, qT)[w][:, :, cols(hf)], parts[:, w, 0, :, cols(hf)],
                                ALU.subtract).then_inc(res_ready, 1)
                dve.wait_ge(mid_ready, i + 1)
                V.tensor_tensor(parts[:, w, 2, :, cols(hf)], resid[:, i % 2], parts[:, w, 1, :, cols(hf)],
                                ALU.subtract).then_inc(lo_ready, 1)

            for i, (w, hf) in enumerate(QK_IDX):
                c, b = cols(hf), 4 + 2 * (i % 2)
                dve.wait_ge(qk_ps, i + 1)
                if i >= 2:
                    dve.wait_ge(rope_ready, i - 1)
                m = (tmp, tmp_odd)[i % 2]
                V.tensor_tensor(m[:, 0], psum[:, b], rope[:, 0, c], ALU.mult)
                V.tensor_tensor(m[:, 1], psum[:, b + 1], rope[:, 1, c], ALU.mult)
                V.tensor_tensor(m[:, 2], psum[:, b + 1], rope[:, 0, c], ALU.mult)
                V.tensor_tensor(m[:, 3], psum[:, b], rope[:, 1, c], ALU.mult).then_inc(rope_mul, 1)
                if i:
                    split(i - 1)
            split(3)

            def score_side(i, t):
                u, s, _ = place(i, t)
                par, k, pair = t // STEPS % 2, s // 2, STEPS * i + t // 2
                if s % 2:
                    dve.wait_ge(sc_ps, pair + 1)
                    V.tensor_reduce(mx[:, par, k:k + 1], banks(2 * (k % 2), 2), AX.X, ALU.max).then_inc(max_ready, 1)
                if s == STEPS - 1:
                    dve.wait_ge(max_ready, pair + 1)
                    V.tensor_copy(mhl[:, 0], mx[:, par]).then_inc(mhl_ready, 1)
                    dve.wait_ge(mhl_ready, 2 * u + 1)
                    V.tensor_tensor(mhl[:, 1], mx[:, par], mhl[:, 0], ALU.subtract).then_inc(mhl_ready, 1)
                if s == 5 and t > 5:
                    max_turned(u - 1)

            def max_turned(u):
                dve.wait_ge(mT_ps, u + 1)
                dve.wait_ge(mrow_in, 32 * u)
                V.tensor_copy(mT, psum[0:32, 7, 0:P // 2].bitcast(BF16)).then_inc(mT_ready, 1)

            tv = tmp.rearrange("p (b h) c -> p b (h c)", b=HB)

            def minimum(i):
                dve.wait_ge(rope_ready, 4)
                if i == 1:
                    dve.wait_ge(feat_ready, 1)
                V.tensor_scalar(tv, (kT, qT)[i], 0.0, None, ALU.min).then_inc(neg_ready, 1)

            def mask_state():
                dve.wait_ge(st_ps, 4)
                src = psum[:, 4, 0:HB * LW].rearrange("p (b c) -> p b c", b=HB)
                mask = const[:, C_MASK:C_MASK + P]
                V.tensor_tensor(state[:, :, 0:P], src[:, :, 0:P], mask.unsqueeze(1).to_broadcast([P, HB, P]), ALU.mult)
                V.tensor_tensor(state[:, :, P:], src[:, :, P:], mask[:, 0:P:HD].unsqueeze(1).to_broadcast([P, HB, 8]),
                                ALU.mult).then_inc(st_ready, 1)

            def lin_scale(j):
                g0, m = LIN[j][0], len(LIN[j])
                dve.wait_ge(lin_ps, j + 1)
                src = psum[:, LIN_BANK[j], 0:m * LW].rearrange("p (g c) -> p g c", g=m)
                link(V.reciprocal(lin_r[:, 0:m], src[:, :, P:]))
                g = gate_2.rearrange("p a (b h) -> p (a b) h", h=8)[:, g0 % HB:g0 % HB + m]
                link(V.tensor_tensor(lin_g[:, 0:m], lin_r[:, 0:m], g, ALU.mult))
                V.tensor_tensor(lin.rearrange("p n (b h c) -> p (n b) h c", b=HB, c=HD)[:, g0:g0 + m],
                                src[:, :, 0:P].rearrange("p g (h c) -> p g h c", c=HD),
                                lin_g[:, 0:m].unsqueeze(3).to_broadcast([P, m, 8, HD]), ALU.mult).then_inc(lin_ready, 1)

            minimum(0)
            for s in range(LEAD):
                score_side(0, s)
                if s == 7:
                    minimum(1)
                if s == 27:
                    mask_state()
                if s - 2 in LIN_STEP:
                    lin_scale(LIN_STEP.index(s - 2))
            lin_scale(len(LIN) - 1)

            def mix(u, qd, hf):
                o = psum[:, 7].rearrange("p (b j c) -> p b j c", b=4, j=4)
                dve.wait_ge(oT_ps, u + 1)
                V.reciprocal(den_r, o[:, :, :, HD]).then_inc(oT_read, 1)
                dve.wait_ge(oT_read, 4 * u + 1)
                om = omg.rearrange("p (q j) -> p q j", q=NQ)[:, qd]
                V.tensor_tensor(den_g, den_r, om.unsqueeze(1).to_broadcast([P, 4, 4]), ALU.mult).then_inc(oT_read, 1)
                dve.wait_ge(oT_read, 4 * u + 2)
                dst = comb.rearrange("p n (q c) -> p q n c", q=NQ)[:, qd]
                V.tensor_tensor(dst.rearrange("p n (j c) -> p n j c", c=HD), o[:, :, :, 0:HD],
                                den_g.unsqueeze(3).to_broadcast([P, 4, 4, HD]), ALU.mult).then_inc(oT_read, 1)
                dve.wait_ge(oT_read, 4 * u + 3)
                src = lin[:, 4 * hf:4 * hf + 4].rearrange("p n (q c) -> p q n c", q=NQ)[:, qd]
                V.tensor_tensor(dst, dst, src, ALU.add).then_inc(oT_read, 1)

            def add_x(hf, n):
                dve.wait_ge(wo_ps, 2 * hf + n + 1)
                c = slice(4 * hf + 2 * n, 4 * hf + 2 * n + 2)
                V.tensor_tensor(x[:, c], x[:, c], psum[:, bank(hf, 2 + n)].rearrange("p (n c) -> p n c", n=2),
                                ALU.add).then_inc(x2_ready, 1)
                dve.wait_ge(x2_ready, 2 * hf + n + 1)
                for m in range(c.start, c.stop):
                    ins = V.bn_stats(stat[:, m], x[:, m])
                if n == 1:
                    link(ins)

            def second_norm(hf):
                dve.wait_ge(rstd_ready, 5 + hf)
                if hf:
                    dve.wait_ge(scattered[0], 16 * K * 4)
                else:
                    dve.wait_ge(xg_filled, 16 * (E + 1))
                for k in range(K):
                    for n in range(4):
                        m = 4 * hf + n
                        V.tensor_scalar(xn2[:, n, k, 0:H], x[:, m], mv[:, m, 0:1], rstd[:, m:m + 1],
                                        ALU.subtract, ALU.mult).then_inc(xn2_ready, 1)

            def choose(hf):
                dve.wait_ge(lg_ps, hf + 1)
                V.tensor_copy(lg, psum[:, bank(hf, 6), 0:4 * E].rearrange("p (n e) -> p n e", e=E)).then_inc(lg_read, 1)
                dve.wait_ge(lg_read, hf + 1)
                for n in range(4):
                    ins = V.max(top[:, n], lg[:, n])
                link(ins)
                V.tensor_tensor(pw_d, top[:, :, 1], top[:, :, 0], ALU.subtract).then_inc(top_ready, 1)
                for n in range(4):
                    ins = V.max_index(topi[:, n], top[:, n], lg[:, n])
                link(ins)
                link(V.tensor_copy(topf, topi[:, :, 0:K]))
                iota = const[:, C_IOTA:C_IOTA + E].unsqueeze(1).to_broadcast([P, 4, E])
                for k in range(K):
                    ins = V.tensor_tensor(onehot[:, k], topf[:, :, k:k + 1].to_broadcast([P, 4, E]), iota, ALU.is_equal)
                link(ins)
                V.tensor_tensor(chosen[:, 4 * hf:4 * hf + 4], onehot[:, 0], onehot[:, 1], ALU.add).then_inc(chosen_ready, 1)

            def place_rows(hf):
                dve.wait_ge(pexp_ready, hf + 1)
                link(V.tensor_scalar(pw_s, pw_e, 1.0, None, ALU.add))
                link(V.reciprocal(xn2[:, :, 0, H], pw_s))
                V.tensor_tensor(xn2[:, :, 1, H], xn2[:, :, 0, H], pw_e, ALU.mult)
                for k in range(K):
                    V.tensor_copy(xn2[:, :, k, H + 1].bitcast(U32), const[:, C_TOK + 4 * hf:C_TOK + 4 * hf + 4])
                dve.wait_ge(rank_ps, hf + 1)
                link(V.tensor_tensor(pos, psum[:, bank(hf, 7), 0:4 * E].rearrange("p (n e) -> p n e", e=E),
                                     const[:, C_LIST:C_LIST + E].unsqueeze(1).to_broadcast([P, 4, E]), ALU.add))
                for k in range(K):
                    ins = V.tensor_tensor(sel[:, k], onehot[:, k], pos, ALU.mult)
                link(ins)
                link(V.tensor_reduce(slot_f, sel, AX.X, ALU.add))
                V.tensor_copy(slot[:, hf], slot_f).then_inc(slot_ready, 1)

            def early_tiles():
                but_last = const[:, C_LTI + (E - 2) * E:C_LTI + (E - 1) * E]
                link(V.tensor_copy(cnt, psum[:, 7, 4 * E:5 * E]))
                link(V.scalar_tensor_tensor(out=full, in0=cnt, scalar=float(P), in1=but_last,
                                            op0=ALU.is_ge, op1=ALU.mult))
                link(V.tensor_tensor(cmp, full.unsqueeze(1).to_broadcast([P, E, E]),
                                     const[:, C_LTI:C_LTI + E * E].rearrange("p (e j) -> p e j", e=E), ALU.mult))
                link(V.tensor_reduce(cum_0, cmp, AX.X, ALU.add))
                V.memset(take[:, E:], 0.0)
                V.scalar_tensor_tensor(out=take[:, 0:E], in0=cum_0, scalar=float(EARLY), in1=full,
                                       op0=ALU.is_le, op1=ALU.mult)
                link(V.tensor_tensor(tau_0, cum_0.unsqueeze(1).to_broadcast([P, EARLY, E]),
                                     const[:, C_TAU:C_TAU + EARLY * E].rearrange("p (n e) -> p n e", e=E), ALU.is_le))
                link(V.tensor_reduce(ex_0, tau_0, AX.X, ALU.add))
                V.tensor_scalar(ex_i[:, 0:EARLY], ex_0, float(E - 2), None, ALU.min).then_inc(early_ready, 1)
                V.tensor_scalar(row_i[:, 0:EARLY], ex_0, float(T), None, ALU.mult).then_inc(early_ready, 1)

            def steps(i, t):
                u, r, n = place(i, t)
                if not (isinstance(n, int) and n + LEAD >= ALL):
                    score_side(i, t + LEAD)
                elif n + LEAD == ALL + 5:
                    max_turned(UNITS - 1)
                if r == 10 and t > 10:
                    unit = u - 1
                    mix(unit, (u + 3) % NQ, 0 if not isinstance(n, int) or unit < NQ else 1)
                if isinstance(n, int) and n in POST:
                    _, f, k = POST[n]
                    if f == "add":
                        add_x(0, k)
                        if k == 1:
                            spreads(0, 4)
                    if f == "norm":
                        second_norm(0)
                    if f == "choose":
                        choose(0)
                    if f == "place":
                        early_tiles()
                        place_rows(0)

            def xgT_copy(t, par):
                dve.wait_ge(xgT_ps, t + 1)
                V.tensor_copy(meta[:, par], xg[:, par, H:ROW].bitcast(U32))
                V.tensor_copy(xgT[:, par], psum[:, 7, 0:HB * P].rearrange("p (b c) -> p b c", b=HB)).then_inc(xgT_ready, 1)

            attention(dve, steps)
            mix(UNITS - 1, NQ - 1, 1)
            xgT_copy(0, 0)
            add_x(1, 0)
            add_x(1, 1)
            spreads(4, 8)
            dve.wait_ge(xgT_ready, 1)
            V.tensor_copy(meta_y[:, 0], meta[:, 0])
            xgT_copy(1, 1)
            second_norm(1)
            choose(1)
            place_rows(1)

            link(V.tensor_copy(cnt, psum[:, 4, 0:E]))
            link(V.tensor_tensor(cmp, cnt.unsqueeze(2).to_broadcast([P, E, E]),
                                 const[:, C_J:C_J + E * E].rearrange("p (e j) -> p e j", e=E), ALU.is_gt))
            link(V.tensor_reduce(tiles, cmp, AX.X, ALU.add))
            V.scalar_tensor_tensor(out=delta, in0=take[:, 1:E + 1], scalar=float(TT), in1=tiles,
                                   op0=ALU.add, op1=ALU.subtract)
            link(V.tensor_tensor(left_tiles, tiles, take[:, 0:E], ALU.subtract))
            link(V.tensor_tensor(cmp, left_tiles.unsqueeze(1).to_broadcast([P, E, E]),
                                 const[:, C_LTI:C_LTI + E * E].rearrange("p (e j) -> p e j", e=E), ALU.mult))
            link(V.tensor_reduce(cum, cmp, AX.X, ALU.add))
            link(V.tensor_tensor(even, cum[:, E - 1:E].to_broadcast([P, PAIRS]), const[:, C_EVEN:C_EVEN + PAIRS],
                                 ALU.is_ge))
            link(V.tensor_reduce(pairs_f, even, AX.X, ALU.add))
            V.tensor_copy(pairs_i[:, 0:1], pairs_f)
            link(V.scalar_tensor_tensor(out=left_f, in0=pairs_f, scalar=-2.0, in1=cum[:, E - 1:E],
                                        op0=ALU.mult, op1=ALU.add))
            V.tensor_scalar(pairs_i[:, 1:2], left_f, float(EARLY - 1), None, ALU.add)
            link(V.tensor_tensor(tau, cum.unsqueeze(1).to_broadcast([P, NTILE + 1, E]),
                                 const[:, C_TAU:].rearrange("p (n e) -> p n e", e=E), ALU.is_le))
            V.tensor_reduce(ex_f, tau, AX.X, ALU.add)
            link(V.tensor_tensor(tau_n, tau, delta.unsqueeze(1).to_broadcast([P, NTILE + 1, E]), ALU.mult))
            link(V.tensor_reduce(ex_n, tau_n, AX.X, ALU.add))
            V.tensor_scalar(ex_i[:, EARLY:], ex_f, float(E - 1), None, ALU.min).then_inc(expert_ready, 1)
            link(V.scalar_tensor_tensor(out=ex_r, in0=ex_n, scalar=take[:, 0:1], in1=const[:, C_ROW0:C_ROW0 + NTILE + 1],
                                        op0=ALU.add, op1=ALU.add))
            V.tensor_scalar(row_i[:, EARLY:], ex_r, float(P), float(E * T), ALU.mult, ALU.min).then_inc(expert_ready, 1)

            def hidden(t, par):
                dve.wait_ge(silu_ready, t + 1)
                V.tensor_tensor(hid[:, par].rearrange("p (b c) -> p b c", b=2),
                                act_g[:, par].rearrange("p (b c) -> p b c", b=2),
                                psum[:, 2:4, 0:FN], ALU.mult).then_inc(hid_ready, 1)

            def hidT_copy(t, par):
                dve.wait_ge(hidT_ps, t + 1)
                V.tensor_copy(hidT[:, par, 0:4], psum[:, 4].rearrange("p (c t) -> p c t", c=4))
                V.tensor_copy(hidT[0:FB[4], par, 4:6], psum[0:FB[4], 5, 0:2 * P].rearrange("p (c t) -> p c t", c=2)
                              ).then_inc(hidT_ready, 1)

            dve.wait_ge(expert_ready, 2)
            pairs = dve.value_load(pairs_i[0:1, 0:1], min_val=1, max_val=PAIRS)
            left = dve.value_load(pairs_i[0:1, 1:2], min_val=0, max_val=1)
            hidden(0, 0)
            hidT_copy(0, 0)
            def take_meta(t, par):
                dve.wait_ge(y_added, 16 * (t - 1))
                dve.wait_ge(xgT_ready, t + 1)
                V.tensor_copy(meta_y[:, par], meta[:, par])

            with dve.Fori(0, PAIRS) as i:
                with dve.If_lt(dve.to_reg(i), pairs):
                    for r in (1, 2):
                        t = 2 * i + r
                        take_meta(t, r % 2)
                        xgT_copy(t + 1, (r + 1) % 2)
                        hidden(t, r % 2)
                        hidT_copy(t, r % 2)
            with dve.If(left):
                take_meta(2 * pairs + 1, 1)
                hidden(2 * pairs + 1, 1)
                hidT_copy(2 * pairs + 1, 1)

        @block.tensor
        def _(pe):
            def mm(*a, **k):
                return nc.tensor.matmul(*a, **k)

            pe.wait_ge(ident_in, 16)
            for hf in range(2):
                pe.wait_ge(xn_ready, 4 * hf + 4)
                for b in range(HB):
                    for n in range(4):
                        ins = nc.tensor.transpose(psum[:, 2 * hf + b, n * P:(n + 1) * P],
                                                  xn[:, 4 * hf + n, b * P:(b + 1) * P], ident)
                    ins.then_inc(xnT_ps, 1)
            for i, (w, hf) in enumerate(QK_IDX):
                pe.wait_ge(xnT_ready, 2 * hf + 2)
                pe.wait_ge(w_in[w], 16)
                if i >= 2:
                    pe.wait_ge(rope_mul, i - 1)
                for o in range(HB):
                    for b in range(HB):
                        ins = mm(psum[:, 4 + 2 * (i % 2) + o], wqkv[:, w, b, o * P:(o + 1) * P],
                                 xnT[:, b, cols(hf)], start=(b == 0), stop=(b == HB - 1))
                ins.then_inc(qk_ps, 1)
            pe.wait_ge(w_in[2], 16)
            pe.wait_ge(xnT_ready, 4)
            for n in range(TT):
                for b in range(HB):
                    ins = mm(psum[:, n // 2, (n % 2) * H:(n % 2 + 1) * H], xnT[:, b, n * P:(n + 1) * P],
                             wqkv[:, 2, b], start=(b == 0), stop=(b == HB - 1))
                if n % 2:
                    ins.then_inc(v_ps, 1)

            def lin_turn(b, g):
                pe.wait_ge(feat_ready, 1)
                pe.wait_ge(rope_mul, 4)
                for n in range(4):
                    ins = nc.tensor.transpose(psum[:, 4 + 2 * b + g, n * P:(n + 1) * P],
                                              kfeat[:, b, (4 * g + n) * P:(4 * g + n + 1) * P], ident)
                ins.then_inc(kft_ps, 1)

            def lin_state(b, g):
                pe.wait_ge(kft_ready, 2 * b + g + 1)
                pe.wait_ge(ones_set, 2)
                for n in range(4 * g, 4 * g + 4):
                    ins = mm(psum[:, 4, b * LW:(b + 1) * LW], kfeat_tok[:, n, b * P:(b + 1) * P], v[:, n, b],
                             start=(n == 0), stop=(n == TT - 1))
                ins.then_inc(st_ps, 1)

            def lin_out(j):
                if j == 0:
                    pe.wait_ge(feat_ready, 2)
                    pe.wait_ge(st_ready, 1)
                if j == 3:
                    pe.wait_ge(mT_ready, 1)
                if j > 3:
                    pe.wait_ge(lin_ready, j - 1)
                for k, g in enumerate(LIN[j]):
                    n, b = g // HB, g % HB
                    ins = mm(psum[:, LIN_BANK[j], k * LW:(k + 1) * LW], qfeat[:, b, n * P:(n + 1) * P],
                             state[:, b], start=True, stop=True)
                ins.then_inc(lin_ps, 1)

            def score(i, t):
                u, s, _ = place(i, t)
                k, kh = s // 2, s % 2
                j, qb = k // 4, k % 4
                pair = STEPS * i + t // 2
                if s == 0:
                    pe.wait_ge(q_in, 16 * GROUPS * (u + 1))
                if kh == 0 and t >= 4:
                    pe.wait_ge(max_ready, pair - 1)
                ins = mm(psum[:, 2 * (k % 2) + kh], qst[0:SROWS, u % 4, j, qb * P:(qb + 1) * P],
                         kst[0:SROWS, u % NQ, j, cols(kh)], start=True, stop=True)
                if kh:
                    ins.then_inc(sc_ps, 1)

            def turn_max(u, first=False):
                pe.wait_ge(mhl_ready, 2 * u + 2)
                nc.tensor.transpose(psum[0:32, 7, 0:P // 2].bitcast(BF16),
                                    mhl.rearrange("p s k -> p (s k)"), ident_b).then_inc(mT_ps, 1)

            def score_t(i, t):
                u, r, n = place(i, t)
                kb, j = r // 4, r % 4
                if r == 0:
                    pe.wait_ge(mrow_in, 32 * (u + 1))
                if isinstance(n, int) and n >= LAST + 4:
                    pe.wait_ge(exp_ready, n - 3)
                elif isinstance(n, int) and n >= LAST:
                    pe.wait_ge(max_ready, STEPS // 2 * UNITS)
                elif t >= 2:
                    pe.wait_ge(exp_ready, n - 1)
                mm(psum[:, score_bank(n, t)], kst[0:SROWS + 2, u % NQ, j, kb * P:(kb + 1) * P],
                   qst[0:SROWS + 2, u % 4, j], start=True, stop=True).then_inc(sct_ps, 1)

            def product(i, g):
                u, kb = 2 * i + g // 8, g % 8
                pe.wait_ge(exp_ready, 2 * STEPS * i + 4 * g + 4)
                if kb == 0:
                    if g:
                        pe.wait_ge(osb_ready, u)
                    pe.wait_ge(v_staged, u + 1)
                for j in range(4):
                    ins = mm(psum[32 * j:32 * j + 32, 6], vst[:, g // 8 % 2, kb, j], prob[:, (4 * g + j) % 8],
                             start=(kb == 0), stop=(kb == 7), skip_group_check=True)
                ins.then_inc(av_ps, 1)

            def turn_o(u, par):
                pe.wait_ge(osb_ready, u + 1)
                pe.wait_ge(mT_ready, u + 2 if not isinstance(u, int) else min(u + 2, UNITS))
                if isinstance(u, int) and u == NQ:
                    pe.wait_ge(x2_ready, 2)
                if isinstance(u, int) and u == NQ + 1:
                    pe.wait_ge(slot_ready, 1)
                for b in range(4):
                    ins = nc.tensor.transpose(psum[:, 7, b * P:(b + 1) * P], osb[:, par, b * P:(b + 1) * P], ident)
                ins.then_inc(oT_ps, 1)

            def project(hf, k, blocks):
                for n in range(2):
                    for b in blocks:
                        ins = mm(psum[:, bank(hf, 2 + k), n * H:(n + 1) * H],
                                 combT[:, b, (2 * k + n) * P:(2 * k + n + 1) * P], wo[:, b],
                                 start=(n == b == 0), stop=(b == HB - 1), skip_group_check=True)
                return ins

            def post(hf, f, k):
                if f == "combT":
                    if hf:
                        pe.wait_ge(oT_read, 4 * (NQ + 2 * k + 2))
                        pe.wait_ge(exp_ready, LAST)
                    else:
                        pe.wait_ge(oT_read, 4 * NQ)
                        if k:
                            pe.wait_ge(combT_ready, 1)
                    for n in range(4):
                        ins = nc.tensor.transpose(psum[:, bank(hf, k), n * P:(n + 1) * P],
                                                  comb[:, n, k * P:(k + 1) * P], ident)
                    ins.then_inc(combT_ps, 1)
                if f == "wo":
                    blocks = range(HB) if not hf else (0,)
                    pe.wait_ge(combT_ready, 2 * hf + len(blocks))
                    pe.wait_ge(wo_in, 16)
                    if k and not hf:
                        pe.wait_ge(mT_ready, NQ + 2)
                    ins = project(hf, k, blocks)
                    if not hf:
                        ins.then_inc(wo_ps, 1)
                if f == "xn2T":
                    b = k - 2
                    pe.wait_ge(xn2_ready, 8 * hf + 4)
                    if not hf:
                        pe.wait_ge(xn2T_ready, 1) if b else pe.wait_ge(oT_read, 4 * (NQ + 1))
                    for n in range(4):
                        ins = nc.tensor.transpose(psum[:, bank(hf, 4 + b), n * P:(n + 1) * P],
                                                  xn2[:, n, 0, b * P:(b + 1) * P], ident)
                    ins.then_inc(xn2T_ps, 1)
                if f == "logits":
                    pe.wait_ge(xn2T_ready, 2 * hf + 2)
                    pe.wait_ge(router_in, 16)
                    for n in range(4):
                        for b in range(HB):
                            ins = mm(psum[:, bank(hf, 6), n * E:(n + 1) * E], xn2T[:, b, n * P:(n + 1) * P],
                                     router[:, b], start=(b == 0), stop=(b == HB - 1))
                    ins.then_inc(lg_ps, 1)
                if f == "rank":
                    if not hf:
                        pe.wait_ge(mT_ready, NQ + 3)
                    pe.wait_ge(chosen_ready, hf + 1)
                    o = psum[:, bank(hf, 7), 0:4 * E]
                    c = chosen[:, 4 * hf:4 * hf + 4].rearrange("p n e -> p (n e)")
                    mm(o, tri_b, c, start=True, stop=False)
                    for n in range(4 * hf + 3):
                        m = max(n - 4 * hf + 1, 0)
                        ins = mm(o[:, m * E:].rearrange("p (n e) -> p n e", e=E), ones_b,
                                 chosen[:, n:n + 1].to_broadcast([P, 4 - m, E]), start=False,
                                 stop=(n == 4 * hf + 2))
                    o = psum[:, 4, 0:E] if hf else psum[:, 7, 4 * E:5 * E]
                    for n in range(4 * hf + 4):
                        ins = mm(o, ones_b, chosen[:, n], start=(n == 0), stop=(n == 4 * hf + 3))
                    ins.then_inc(rank_ps, 1)

            pe.wait_ge(kst_set, 1)
            pe.wait_ge(identb_ready, 1)
            pe.wait_ge(v_ready, 4)
            pe.wait_ge(k0_in, 16 * GROUPS)
            for s in range(LEAD):
                score(0, s)
                if s in (11, 13, 15, 17):
                    lin_turn((s - 11) // 4, (s - 11) // 2 % 2)
                if s in (19, 21, 23, 25):
                    lin_state((s - 19) // 4, (s - 19) // 2 % 2)
                if s == 35:
                    pe.wait_ge(kft_ready, 4)
                    turn_max(0)
                if s in LIN_STEP:
                    lin_out(LIN_STEP.index(s))
            pe.wait_ge(lin_ready, 2)
            pe.wait_ge(ones_set, 3)

            def steps(i, t):
                u, r, n = place(i, t)
                score_t(i, t)
                if not (isinstance(n, int) and n + LEAD >= ALL):
                    score(i, t + LEAD)
                if t == 4:
                    pe.wait_ge(lin_ready, 5)
                if t % 4 == 1 and t > 1:
                    product(i, t // 4 - 1)
                if r == 8 and t > 8:
                    turn_o(u - 1, (t // STEPS - 1) % 2)
                if (t + LEAD) % STEPS == 3:
                    m = 2 * i + (t + LEAD) // STEPS - 1
                    if not (isinstance(n, int) and n + LEAD > ALL + 3):
                        pe.wait_ge(oT_read, 4 * (m - 1))
                        pe.wait_ge(lin_ready, 6)
                        if isinstance(m, int) and m == NQ + 1:
                            pe.wait_ge(x2_ready, 1)
                        if isinstance(m, int) and m == NQ + 2:
                            pe.wait_ge(lg_read, 1)
                        turn_max(m)
                if isinstance(n, int) and n in POST:
                    post(*POST[n])

            def load_expert(t):
                return pe.value_load(ex_i[0:1, bass.ts(t, 1)], min_val=0, max_val=E - 1)

            def columns(par, e, chunks):
                for c in chunks:
                    for b in range(HB):
                        ins = mm(psum[:, c, 0:FN], xgT[:, par, b], gu[:, e, b, c * FN:(c + 1) * FN],
                                 start=(b == 0), stop=(b == HB - 1))
                return ins

            def gate_up(t, par, e):
                pe.wait_ge(xgT_ready, t + 1)
                pe.wait_ge(hid_ready, t)
                columns(par, e, range(4)).then_inc(gu_ps, 1)

            def turn_x(par, loads):
                pe.wait_ge(xg_in[par], 16 * loads)
                for b in range(HB):
                    ins = nc.tensor.transpose(psum[:, 7, b * P:(b + 1) * P], xg[:, par, b * P:(b + 1) * P], ident)
                ins.then_inc(xgT_ps, 1)

            attention(pe, steps)
            product(NQ // 2, NQ * STEPS // 4 - 1)
            pe.wait_ge(oT_read, 4 * (UNITS - 1))
            turn_o(UNITS - 1, 1)
            post(1, "combT", 1)
            turn_x(0, 1)
            pe.wait_ge(combT_ready, 4)
            for k in range(2):
                project(1, k, (1,)).then_inc(wo_ps, 1)
            pe.wait_ge(xgT_ready, 1)
            turn_x(1, 1)
            pe.wait_ge(early_ready, 2)
            pe.wait_ge(gu_in, 16 * (E - 1))
            e0 = load_expert(0)
            columns(0, e0, (0, 1))
            post(1, "xn2T", 2)
            post(1, "xn2T", 3)
            post(1, "logits", 0)
            columns(0, e0, (2,))
            post(1, "rank", 0)
            columns(0, e0, (3,)).then_inc(gu_ps, 1)

            def turn_hidden(t, par):
                pe.wait_ge(hid_ready, t + 1)
                for c, (o, n) in enumerate(zip(FO, FB)):
                    ins = nc.tensor.transpose(psum[0:n, 4 + c // 4, (c % 4) * P:(c % 4 + 1) * P],
                                              hid[:, par, o:o + n], ident)
                ins.then_inc(hidT_ps, 1)

            def down(t, par, e):
                pe.wait_ge(hidT_ready, t + 1)
                pe.wait_ge(y_ready, t)
                for c, n in enumerate(FB):
                    ins = mm(psum[:, 6, 0:H], hidT[0:n, par, c], dn[0:n, c, e], start=(c == 0),
                             stop=(c == len(FB) - 1))
                ins.then_inc(y_ps, 1)

            pe.wait_ge(expert_ready, 2)
            pairs = pe.value_load(pairs_i[0:1, 0:1], min_val=1, max_val=PAIRS)
            left = pe.value_load(pairs_i[0:1, 1:2], min_val=0, max_val=1)
            turn_hidden(0, 0)
            pe.wait_ge(gu_in, 16 * E)
            pe.wait_ge(dn_in, 16 * len(FB))
            with pe.Fori(0, PAIRS) as i:
                with pe.If_lt(pe.to_reg(i), pairs):
                    t = 2 * i + 1
                    e1 = load_expert(t)
                    gate_up(t, 1, e1)
                    turn_x(0, i + 2)
                    down(t - 1, 0, load_expert(t - 1))
                    e2 = load_expert(t + 1)
                    turn_hidden(t, 1)
                    gate_up(t + 1, 0, e2)
                    turn_x(1, i + 2)
                    down(t, 1, e1)
                    turn_hidden(t + 1, 0)
            with pe.If(left):
                gate_up(2 * pairs + 1, 1, load_expert(2 * pairs + 1))
            down(2 * pairs, 0, load_expert(2 * pairs))
            with pe.If(left):
                turn_hidden(2 * pairs + 1, 1)
                down(2 * pairs + 1, 1, load_expert(2 * pairs + 1))


def kernel(**inputs):
    from concourse import bacc
    from concourse.bass_utils import run_bass_kernel_spmd

    f = {n.removeprefix("L0_"): np.asarray(a) for n, a in inputs.items()}
    rows = lambda w: w.T.reshape(HB, P, -1).transpose(1, 0, 2)
    weights = np.stack([rows(f[n]) for n in ("attn_Wk", "attn_Wq", "attn_Wv", "attn_Wo")], 1)
    gate_up = np.concatenate([f["ffn_gate_w"], f["ffn_up_w"]], 1)
    const, rope = constants()
    arrays = {
        "x": f["attn_hidden_states"],
        "weights": weights,
        "rope": rope,
        "const": const,
        "gate": f["attn_gate"].reshape(1, NH),
        "router": rows(f["ffn_router_w"]),
        "gate_up": gate_up.transpose(2, 0, 1).reshape(HB, P, E, 2 * F).transpose(1, 2, 0, 3),
        "down": f["ffn_down_w"].transpose(2, 0, 1),
    }
    arrays = {n: np.ascontiguousarray(a) for n, a in arrays.items()}
    nc = bacc.Bacc("TRN2", target_bir_lowering=False, num_devices=1)
    args = [nc.dram_tensor(n, a.shape, mybir.dt.from_np(a.dtype), kind="ExternalInput").ap()
            for n, a in arrays.items()]
    args.append(nc.dram_tensor("out", [1, T, H], F32, kind="ExternalOutput").ap())
    block_kernel(nc, *args)
    return run_bass_kernel_spmd(nc, [arrays], core_ids=[0]).results[0]["out"]
```
